# Optimizing a Trainium2 kernel written in Bass

```python
import numpy as np
import jax
import jax.numpy as jnp

def _softmax(x, axis=-1):
    return jax.nn.softmax(x, axis=axis)

def _gelu(x):
    return jax.nn.gelu(x, approximate=True)

def _silu(x):
    return jax.nn.silu(x)

def _sigmoid(x):
    return jax.nn.sigmoid(x)

def _layernorm(x, axis=-1, eps=1e-05):
    m = jnp.mean(x, axis=axis, keepdims=True)
    v = jnp.var(x, axis=axis, keepdims=True)
    return (x - m) / jnp.sqrt(v + eps)

def _scatter_add(tgt, idx, src, axis=0):
    return tgt.at[idx].add(src)

def _segment_sum(src, seg, n):
    return jax.ops.segment_sum(src, seg, n)
kernel_name = 'mk_gnn_resnorm_d2_gnn_r8_f32ec6'

def setup_inputs(seed: int=0):
    np.random.seed(seed)
    _w = jnp.asarray

    def _rec_inputs():
        import jax
        import jax.numpy as jnp
        _gk = jax.random.key(seed)
        x = -0.0003713 + 1 * jax.random.normal(jax.random.fold_in(_gk, 1), (6250, 256), jnp.float32)
        _s = jax.random.randint(jax.random.fold_in(_gk, 2), (50000,), 0, 6250, jnp.int32)
        _d = jax.random.randint(jax.random.fold_in(_gk, 3), (50000,), 0, 6250, jnp.int32)
        _loop = jnp.arange(6250, dtype=jnp.int32)
        src = jnp.concatenate([_s, _d, _loop])
        dst = jnp.concatenate([_d, _s, _loop])
        _o = jnp.argsort(dst, stable=True)
        src = src[_o]
        dst = dst[_o]
        edge_weight1 = jax.random.uniform(jax.random.fold_in(_gk, 12), (106250, 1), jnp.float32, 0.0, 0.999998)
        return (x, src, dst, edge_weight1)
    x, src, dst, edge_weight1 = _rec_inputs()

    def _L0_gnn_setup():
        import jax, jax.numpy as jnp
        import numpy as np
        N_NODES = 6250
        DIM_H = 256
        N_EDGES = 100000
        LN_EPS = 1e-05

        def _layer_norm(x, g, b):
            mu = jnp.mean(x, axis=-1, keepdims=True)
            var = jnp.mean(jnp.square(x - mu), axis=-1, keepdims=True)
            return (x - mu) * jax.lax.rsqrt(var + LN_EPS) * g + b
        key = jax.random.key(seed)
        ks = jax.random.split(key, 12)
        d = DIM_H

        def lin(k, fan_in, fan_out):
            lim = 1.0 / np.sqrt(fan_in)
            kw, kb = jax.random.split(k)
            W = jax.random.uniform(kw, (fan_in, fan_out), jnp.float32, -lim, lim)
            b = jax.random.uniform(kb, (fan_out,), jnp.float32, -lim, lim)
            return (W, b)
        h = jax.random.normal(ks[0], (N_NODES, d), jnp.float32)
        e = jax.random.randint(ks[1], (2, N_EDGES), 0, N_NODES, jnp.int64)
        d2 = jax.random.uniform(ks[2], (N_EDGES, 1), jnp.float32)
        mW1, mb1 = lin(ks[3], 2 * d + 1, d)
        mW2, mb2 = lin(ks[4], d, d)
        ln_g = jnp.ones((d,), jnp.float32)
        ln_b = jnp.zeros((d,), jnp.float32)
        uW1, ub1 = lin(ks[5], 2 * d, d)
        uW2, ub2 = lin(ks[6], d, d)
        return {'h': h, 'e': e, 'd2': d2, 'mW1': mW1, 'mb1': mb1, 'ln_g': ln_g, 'ln_b': ln_b, 'mW2': mW2, 'mb2': mb2, 'uW1': uW1, 'ub1': ub1, 'uW2': uW2, 'ub2': ub2}
    _L0_gnn_all = _L0_gnn_setup()
    _L0_gnn_in = {k: v for k, v in _L0_gnn_all.items() if k in ('mW1', 'mb1', 'ln_g', 'ln_b', 'mW2', 'mb2', 'uW1', 'ub1', 'uW2', 'ub2')}
    del _L0_gnn_all

    def _L1_gnn_setup():
        import jax, jax.numpy as jnp
        import numpy as np
        DIM = 256
        HIDDEN = 256
        NUM_ENT = 25000
        NUM_TRI = 25000
        NUM_EDGES = 75000
        key = jax.random.key(seed)
        k1, k2, k3, k4, k5 = jax.random.split(key, 5)
        entity_emb = jax.random.normal(k1, (NUM_ENT, DIM), dtype=jnp.float32)
        src_idx = jax.random.randint(k2, (NUM_EDGES,), 0, NUM_ENT, dtype=jnp.int64)
        dst_idx = jax.random.randint(k3, (NUM_EDGES,), 0, NUM_TRI, dtype=jnp.int64)
        entity_triangle_index = jnp.stack([src_idx, dst_idx], axis=0)
        bound = 1.0 / np.sqrt(DIM)
        W = jax.random.uniform(k4, (HIDDEN, DIM), minval=-bound, maxval=bound, dtype=jnp.float32)
        b = jax.random.uniform(k5, (HIDDEN,), minval=-bound, maxval=bound, dtype=jnp.float32)
        return {'entity_emb': entity_emb, 'entity_triangle_index': entity_triangle_index, 'num_triangles': NUM_TRI, 'W': W, 'b': b}
    _L1_gnn_all = _L1_gnn_setup()
    _L1_gnn_in = {k: v for k, v in _L1_gnn_all.items() if k in ('W', 'b')}
    del _L1_gnn_all
    return {'x': x, 'src': src, 'dst': dst, 'edge_weight1': edge_weight1, 'L0_gnn_mW1': _L0_gnn_in['mW1'], 'L0_gnn_mb1': _L0_gnn_in['mb1'], 'L0_gnn_ln_g': _L0_gnn_in['ln_g'], 'L0_gnn_ln_b': _L0_gnn_in['ln_b'], 'L0_gnn_mW2': _L0_gnn_in['mW2'], 'L0_gnn_mb2': _L0_gnn_in['mb2'], 'L0_gnn_uW1': _L0_gnn_in['uW1'], 'L0_gnn_ub1': _L0_gnn_in['ub1'], 'L0_gnn_uW2': _L0_gnn_in['uW2'], 'L0_gnn_ub2': _L0_gnn_in['ub2'], 'L1_gnn_W': _L1_gnn_in['W'], 'L1_gnn_b': _L1_gnn_in['b']}

def reference(x, src, dst, edge_weight1, L0_gnn_mW1, L0_gnn_mb1, L0_gnn_ln_g, L0_gnn_ln_b, L0_gnn_mW2, L0_gnn_mb2, L0_gnn_uW1, L0_gnn_ub1, L0_gnn_uW2, L0_gnn_ub2, L1_gnn_W, L1_gnn_b):
    import jax
    import jax.numpy as jnp

    def _L0_gnn_ref(h, e, d2, mW1, mb1, ln_g, ln_b, mW2, mb2, uW1, ub1, uW2, ub2):
        import jax, jax.numpy as jnp
        import numpy as np
        N_NODES = 6250
        DIM_H = 256
        N_EDGES = 100000
        LN_EPS = 1e-05

        def _layer_norm(x, g, b):
            mu = jnp.mean(x, axis=-1, keepdims=True)
            var = jnp.mean(jnp.square(x - mu), axis=-1, keepdims=True)
            return (x - mu) * jax.lax.rsqrt(var + LN_EPS) * g + b
        ei, ej = (e[0], e[1])
        hi = h[ei]
        hj = h[ej]
        x = jnp.concatenate((hi, hj, d2), axis=-1)
        msg = jax.nn.silu(x @ mW1 + mb1)
        msg = _layer_norm(msg, ln_g, ln_b)
        msg = jax.nn.silu(msg @ mW2 + mb2)
        agg = jax.ops.segment_sum(msg, ei, num_segments=h.shape[0])
        y = jnp.concatenate((h, agg), axis=-1)
        y = jax.nn.silu(y @ uW1 + ub1) @ uW2 + ub2
        return h + y

    def _L1_gnn_ref(entity_emb, entity_triangle_index, num_triangles, W, b):
        import jax, jax.numpy as jnp
        import numpy as np
        DIM = 256
        HIDDEN = 256
        NUM_ENT = 25000
        NUM_TRI = 25000
        NUM_EDGES = 75000
        src_idx = entity_triangle_index[0]
        dst_idx = entity_triangle_index[1]
        msgs = entity_emb[src_idx]
        agg = jax.ops.segment_sum(msgs, dst_idx, num_segments=num_triangles)
        counts = jax.ops.segment_sum(jnp.ones((src_idx.shape[0],), dtype=entity_emb.dtype), dst_idx, num_segments=num_triangles)
        agg = jnp.where(counts[:, None] > 0, agg / jnp.maximum(counts, 1.0)[:, None], agg)
        tri_out = jax.nn.relu(agg @ W.T + b)
        return tri_out
    edge_index = jnp.stack([src, dst])
    x = _layernorm(x + _L0_gnn_ref(x, edge_index, edge_weight1, L0_gnn_mW1, L0_gnn_mb1, L0_gnn_ln_g, L0_gnn_ln_b, L0_gnn_mW2, L0_gnn_mb2, L0_gnn_uW1, L0_gnn_ub1, L0_gnn_uW2, L0_gnn_ub2), axis=-1)
    x = _layernorm(x + _L1_gnn_ref(x, edge_index, 6250, L1_gnn_W, L1_gnn_b), axis=-1)
    return x

_drawn_inputs = setup_inputs


def setup_inputs(seed=0):
    import zlib

    import numpy as np

    out = dict(_drawn_inputs(seed))
    spreads = {'L0_gnn_ln_g': (1.0, 0.2), 'L0_gnn_ln_b': (0.0, 0.1)}
    factors = {'edge_weight1': 43.935, 'L0_gnn_mb1': 3.034, 'L0_gnn_ub1': 8.0, 'L0_gnn_ub2': 3.058}
    for name, (base, spread) in spreads.items():
        noise = np.random.default_rng([zlib.crc32(name.encode()), seed]).standard_normal(out[name].shape)
        drawn = base * np.exp(spread * noise) if base else spread * noise
        out[name] = jnp.asarray(drawn.astype(out[name].dtype))
    for name, factor in factors.items():
        out[name] = (out[name] * factor).astype(out[name].dtype)
    return out
```

```python
import concourse.bass as bass
from concourse import mybir
from contextlib import ExitStack

N = 6250
D = 256
E = 106250
P = 128
H = D // P
LN_EPS = 1e-5

QT = 4
QUADS = 208
TILES = QUADS * QT
CHUNKS = -(-TILES // P)
FULL = E // P
REST = E - FULL * P
NB = 125
BLOCKS = N // NB
ROWS = N + NB
PAD = N
SUMROWS = 50 * P
TABLES = QT
CW = 260
MAGIC = 0x5F3759DF
NEWTON = 3
NEWTON_OPS = 4 + 3 * NEWTON
assert TILES * P >= E and BLOCKS * NB == N and SUMROWS >= N + P and REST > 0


def gnn(nc, x, src, dst, edge_w, mW1, mb1, ln_g, ln_b, mW2, mb2, uW1, ub1, uW2, ub2, W, b, out):
    f32, i32, bf16 = mybir.dt.float32, mybir.dt.int32, mybir.dt.bfloat16
    ALU = mybir.AluOpType
    ACT = mybir.ActivationFunctionType

    pq = nc.dram_tensor("pq", (2 * ROWS, D), f32, kind="Internal").ap()
    x1_tab = nc.dram_tensor("x1_tab", (ROWS, D), f32, kind="Internal").ap()
    sums = [[nc.dram_tensor(f"sum{l}_{r}", (SUMROWS, w), f32, kind="Internal").ap() for r in range(TABLES)]
            for l, w in ((0, D), (1, CW))]

    with ExitStack() as ctx:
        def sb(name, shape, dt=f32):
            return ctx.enter_context(nc.sbuf_tensor(name, shape, dt))

        def sem(name):
            return ctx.enter_context(nc.semaphore(name))

        ident = sb("ident", [P, P])
        lower = sb("lower", [P, P])
        zeros = sb("zeros", [P, CW])
        ones = sb("ones", [P, P], bf16)
        xs = sb("xs", [NB, BLOCKS, D])
        w1 = sb("w1", [P, 2 * H, D])
        w2 = sb("w2", [P, H, D])
        u1 = sb("u1", [P, 2 * H, D])
        u2 = sb("u2", [P, H, D])
        wl = sb("wl", [P, H, D])
        wt = sb("wt", [P, H, D])
        w1c = sb("w1c", [P, D])
        b1q = sb("b1q", [P, 2, D])
        b2f = sb("b2f", [P, 3, D])
        b2p = sb("b2p", [P, 3, D], bf16)
        b2r = sb("b2r", [P, D], bf16)
        ub1b = sb("ub1b", [P, D])
        ub2b = sb("ub2b", [P, D])
        blb = sb("blb", [P, D])
        gb = sb("gb", [P, H, 2])
        rec = sb("rec", [P, TILES, 4])
        dstf = sb("dstf", [P, TILES])
        trash_i = sb("trash_i", [P, QT], i32)
        trash = sb("trash", [P, QT])
        mst = sb("mst", [NB, BLOCKS, 2])
        nwb = sb("nwb", [NB, 5, BLOCKS])

        gat = sb("gat", [P, 2, QT, 2, D])
        act = sb("act", [P, 2, QT, D])
        zt = sb("zt", [P, 2, H, QT * P])
        msg = sb("msg", [P, 2, QT, CW])
        same = sb("same", [P, 2, QT, P])
        tot = sb("tot", [P, 2, QT, CW])
        scr = sb("scr", [P, QT, P])
        idx = sb("idx", [P, 2, QT, 2], i32)
        key = sb("key", [P, 2, QT, 2])
        dup = sb("dup", [P, 2, QT])
        dif = sb("dif", [P, 2, QT, 2])
        sidx = sb("sidx", [P, 2, QT], i32)
        bst = sb("bst", [P, 2, QT, 6])
        mom = sb("mom", [P, 2, 5, QT])
        nwt = sb("nwt", [P, 2, 5, QT])
        blk = sb("blk", [P, 2, TABLES, CW])
        half = sb("half", [P, 2, 2, CW])
        agg = sb("agg", [P, 2, CW])
        col = sb("col", [P, 2, 2 * H, P])
        xin = sb("xin", [NB, 2, D])
        hpre = sb("hpre", [P, 2, D])
        hpre2 = sb("hpre2", [P, 2, D])
        hid = sb("hid", [P, 2, D])
        hcol = sb("hcol", [P, 2, H, P])
        cnt = sb("cnt", [P, 2, 2])
        mv2 = sb("mv2", [NB, 2, 2])
        bst2 = sb("bst2", [NB, 2, 6])
        loaded = gat[:, :, :, :, :].rearrange("p a b c d -> p (a b c d)")[:, 0:3 * CHUNKS * P]\
            .rearrange("p (a k e) -> p a k e", a=3, k=CHUNKS)
        ends = act[:, :, :, :].rearrange("p a b c -> p (a b c)")[:, 0:2 * CHUNKS * P]\
            .rearrange("p (a k e) -> p a k e", a=2, k=CHUNKS)

        ps = ctx.enter_context(nc.psum_tensor("ps", [P, 8, 512], f32))
        PM, PZ, PD, PK, PO = 0, 2, 4, 6, 7

        def flat(ap):
            return ap.rearrange("p a b -> p (a b)")

        s_const, s_constc, s_zeroed, s_pad = sem("s_const"), sem("s_constc"), sem("s_zeroed"), sem("s_pad")
        s_edges, s_weights, s_x, s_tables = sem("s_edges"), sem("s_weights"), sem("s_x"), sem("s_tables")
        s_ends, s_etr, s_rec, s_recc = sem("s_ends"), sem("s_etr"), sem("s_rec"), sem("s_recc")
        s_bias, s_wtr, s_wt = sem("s_bias"), sem("s_wtr"), sem("s_wt")
        s_xt, s_xtev, s_pqmm, s_pqrow = sem("s_xt"), sem("s_xtev"), sem("s_pqmm"), sem("s_pqrow")
        s_pqst = [sem("s_pqst0"), sem("s_pqst1")]
        s_xin, s_biasr, s_dturn = sem("s_xin"), sem("s_biasr"), sem("s_dturn")
        s_turn = sem("s_turn")
        s_x1st, s_out, s_ones = sem("s_x1st"), sem("s_out"), sem("s_ones")
        s_done = [sem("s_x1done"), sem("s_x2done")]

        EDGE = ["staged", "gat0", "gat1", "prea", "pre", "silu", "bst", "mom", "newt", "norm", "keyt", "same",
                "dup", "dif", "sidx", "ztr", "zev", "mm", "msg", "ded", "tot", "totv", "added"]
        e = [{n: sem(f"e{l}_{n}") for n in EDGE} for l in range(2)]
        BLOCK = ["load0", "load1", "half", "agg", "cnt", "cols", "colev", "hmm", "hpre", "hid", "hcols", "hcolev",
                 "omm", "oadd", "res", "bst", "stat", "newt", "norm", "xin", "aggr"]
        k = [{n: sem(f"b{l}_{n}") for n in BLOCK} for l in range(2)]

        block = ctx.enter_context(nc.Block())

        def steps(eng, n, lag, step, ahead=0):
            lo = 4
            hi = (n - ahead) // 2 * 2
            for q in range(lo):
                step(q, q % 2)
            with eng.Fori(lo // 2, hi // 2) as it:
                for par in (0, 1):
                    step(it * 2 + par, par)
            for q in range(hi, n + lag):
                step(q, q % 2)

        def live(q, n):
            return not isinstance(q, int) or 0 <= q < n

        def half_count(q):
            return q // 2 + 1

        def later(q, n):
            return not isinstance(q, int) or q >= n

        def inverse_root(dve, v, w, sem_, at):
            nc.vector.tensor_scalar(w[0], v, LN_EPS, None, ALU.add).then_inc(sem_, 1)
            nc.vector.tensor_scalar(w[1], v, LN_EPS, -0.5, ALU.add, ALU.mult).then_inc(sem_, 1)
            dve.wait_ge(sem_, at + 1)
            nc.vector.tensor_scalar(w[2].bitcast(i32), w[0].bitcast(i32), 1, None, ALU.logical_shift_right)\
                .then_inc(sem_, 1)
            dve.wait_ge(sem_, at + 3)
            nc.vector.tensor_scalar(w[4].bitcast(i32), w[2].bitcast(i32), -1.0, float(MAGIC), ALU.mult, ALU.add)\
                .then_inc(sem_, 1)
            for i in range(NEWTON):
                dve.wait_ge(sem_, at + 4 + 3 * i)
                nc.vector.tensor_tensor(w[2], w[4], w[4], ALU.mult).then_inc(sem_, 1)
                dve.wait_ge(sem_, at + 5 + 3 * i)
                nc.vector.tensor_tensor(w[3], w[2], w[1], ALU.mult).then_inc(sem_, 1)
                dve.wait_ge(sem_, at + 6 + 3 * i)
                nc.vector.scalar_tensor_tensor(out=w[4], in0=w[3], scalar=1.5, in1=w[4], op0=ALU.add, op1=ALU.mult)\
                    .then_inc(sem_, 1)

        @block.sync
        def _(sp):
            sp.wait_ge(s_pad, 2)
            last, left = CHUNKS - 1, FULL - (CHUNKS - 1) * P
            for a, arr in enumerate((src, dst, edge_w.rearrange("e o -> (e o)"))):
                dest = loaded[:, a] if a == 2 else loaded[:, a].bitcast(i32)
                sp.dma_start(dest[:, 0:last, :], arr[0:last * P * P].rearrange("(k r e) -> r k e", r=P, e=P))\
                    .then_inc(s_edges, 16)
                sp.dma_start(dest[0:left, last, :], arr[last * P * P:FULL * P].rearrange("(r e) -> r e", e=P))\
                    .then_inc(s_edges, 16)
                sp.dma_start(dest[left:left + 1, last, 0:REST], arr[FULL * P:E].rearrange("(r e) -> r e", e=REST))\
                    .then_inc(s_edges, 16)
            sp.dma_start(xs[:, :, :], x.rearrange("(j p) d -> p j d", p=NB)).then_inc(s_x, 16)
            for dest, arr in ((w1, mW1[0:2 * D, :]), (w2, mW2), (u1, uW1), (u2, uW2), (wl, W)):
                sp.dma_start(dest[:, :, :], arr.rearrange("(k p) d -> p k d", p=P)).then_inc(s_weights, 16)
            for dest, row in ((w1c[:, :], mW1[2 * D:2 * D + 1, :]), (b1q[:, 0, :], mb1), (b2f[:, 0, :], mb2),
                              (ub1b[:, :], ub1), (ub2b[:, :], ub2), (blb[:, :], b)):
                row = row if len(row.shape) == 2 else row.rearrange("(a n) -> a n", a=1)
                sp.dma_start(dest, row.to_broadcast([P, D])).then_inc(s_weights, 16)
            for a, row in enumerate((ln_g, ln_b)):
                for h in range(H):
                    sp.dma_start(gb[:, h, a:a + 1], row[h * P:(h + 1) * P].rearrange("(p a) -> p a", a=1))\
                        .then_inc(s_weights, 16)
            sp.wait_ge(s_zeroed, 2)
            for tabs, width in ((sums[0], D), (sums[1], CW)):
                for t in tabs:
                    sp.dma_start(t.rearrange("(p a) d -> p a d", p=P),
                                 zeros[:, 0:width].unsqueeze(1).to_broadcast([P, SUMROWS // P, width]))\
                        .then_inc(s_tables, 16)
            sp.dma_start(pq[2 * N:2 * ROWS, :].rearrange("(p a) d -> p a d", a=2),
                         zeros[0:NB, 0:D].unsqueeze(1).to_broadcast([NB, 2, D])).then_inc(s_tables, 16)
            sp.dma_start(x1_tab[N:ROWS, :], zeros[0:NB, 0:D]).then_inc(s_tables, 16)

            def store_pq(q, par):
                sp.wait_ge(s_pqrow, q + 1)
                sp.dma_start(pq[bass.ds(q * (2 * NB), 2 * NB), :].rearrange("(p a) d -> p a d", a=2),
                             msg[0:NB, par, 0:2, 0:D]).then_inc(s_pqst[par], 16)
            steps(sp, BLOCKS, 0, store_pq)

            for l, width in ((0, D), (1, CW)):
                sp.wait_ge(e[l]["added"], 16 * QT * QUADS)

                def load_sums(q, par):
                    if later(q, 2):
                        sp.wait_ge(k[l]["half"], q - 1)
                    for r in range(TABLES):
                        sp.dma_start(blk[0:NB, par, r, 0:width], sums[l][r][bass.ds(q * NB, NB), :])\
                            .then_inc(k[l][f"load{par}"], 16)
                steps(sp, BLOCKS, 0, load_sums)
                sp.wait_ge(s_done[l], 1)
                if l == 0:
                    sp.dma_start(x1_tab[0:N, :].rearrange("(j p) d -> p j d", p=NB), xs[:, :, :]).then_inc(s_x1st, 16)
                else:
                    sp.dma_start(out.rearrange("(j p) d -> p j d", p=NB), xs[:, :, :]).then_inc(s_out, 16)
            sp.wait_ge(s_out, 16)

        @block.gpsimd
        def _(pool):
            nc.gpsimd.memset(loaded[:, 0:2, CHUNKS - 1, :].bitcast(i32), PAD).then_inc(s_pad, 1)
            nc.gpsimd.memset(loaded[:, 2, CHUNKS - 1, :], 0.0).then_inc(s_pad, 1)
            nc.gpsimd.memset(zeros[:, :], 0.0).then_inc(s_zeroed, 1)
            nc.gpsimd.memset(b1q[:, 1, :], 0.0).then_inc(s_zeroed, 1)
            nc.gpsimd.memset(ident[:, :], 0.0).then_inc(s_constc, 1)
            nc.gpsimd.memset(lower[:, :], 1.0).then_inc(s_constc, 1)
            nc.gpsimd.memset(ones[:, :], 1.0).then_inc(s_const, 1)
            nc.gpsimd.iota(trash_i[:, :], pattern=[[0, QT]], base=N, channel_multiplier=1).then_inc(s_constc, 1)
            pool.wait_ge(s_constc, 3)
            nc.gpsimd.affine_select(out=ident[:, :], in_=ident[:, :], compare_op=ALU.not_equal, fill=1.0, base=0,
                                    pattern=[[-1, P]], channel_multiplier=1).then_inc(s_const, 1)
            nc.gpsimd.affine_select(out=lower[:, :], in_=lower[:, :], compare_op=ALU.is_gt, fill=0.0, base=0,
                                    pattern=[[-1, P]], channel_multiplier=1).then_inc(s_const, 1)
            nc.gpsimd.tensor_copy(trash[:, :], trash_i[:, :]).then_inc(s_const, 1)
            pool.wait_ge(s_pad, 2)
            pool.wait_ge(s_tables, 16 * (2 * TABLES + 2))
            for par in (0, 1):
                pool.wait_ge(s_pqst[par], 16 * BLOCKS // 2)

            for l in range(2):
                if l == 1:
                    pool.wait_ge(s_x1st, 16)

                def gather(q, par):
                    pool.wait_ge(e[l]["staged"], q + 1)
                    if later(q, 2):
                        pool.wait_ge(e[l]["pre" if l == 0 else "ded"], q - 1)
                    pool.sem_inc(s_turn, 1)
                    for u in range(QT):
                        if l == 0:
                            for a in range(2):
                                pool.indirect_dma_start(
                                    out=gat[:, par, u, a, :], out_offset=None, in_=pq[:, :],
                                    in_offset=bass.IndirectOffsetOnAxis(ap=idx[:, par, u, a:a + 1], axis=0))\
                                    .then_inc(e[l][f"gat{par}"], 16)
                        else:
                            pool.indirect_dma_start(
                                out=msg[:, par, u, 0:D], out_offset=None, in_=x1_tab[:, :],
                                in_offset=bass.IndirectOffsetOnAxis(ap=idx[:, par, u, 0:1], axis=0))\
                                .then_inc(e[l][f"gat{par}"], 16)

                def add(q, par):
                    pool.wait_ge(e[l]["tot"], q + 1)
                    pool.wait_ge(e[l]["totv"], q + 1)
                    pool.wait_ge(e[l]["sidx"], q + 1)
                    if later(q, 1):
                        pool.wait_ge(e[l]["added"], q * (16 * QT))
                    pool.sem_inc(s_turn, 1)
                    width = D if l == 0 else CW
                    for u in range(QT):
                        pool.indirect_dma_start(
                            out=sums[l][u][:, :], in_=tot[:, par, u, 0:width], in_offset=None,
                            out_offset=bass.IndirectOffsetOnAxis(ap=sidx[:, par, u:u + 1], axis=0),
                            compute_op=ALU.add).then_inc(e[l]["added"], 16)

                back = 2 if l == 0 else 1

                def step(q, par):
                    if live(q + 1, QUADS):
                        gather(q + 1, 1 - par)
                    if live(q - back, QUADS):
                        add(q - back, (par + back) % 2)
                gather(0, 0)
                steps(pool, QUADS, back, step, ahead=1)

        @block.tensor
        def _(pe):
            pe.wait_ge(s_const, 4)
            pe.wait_ge(s_ends, 1)
            pe.wait_ge(s_edges, 16 * 9)
            for c in range(CHUNKS):
                n = min(P, TILES - c * P)
                if c >= 2:
                    pe.wait_ge(s_rec, c - 1)
                for a in range(3):
                    rows = (ends[0:n, a, c, :] if a < 2 else loaded[0:n, 2, c, :])
                    last = nc.tensor.transpose(ps[:, PZ + c % 2, a * P:a * P + n], rows, ident[0:n, 0:n])
                last.then_inc(s_etr, 1)
            pe.wait_ge(s_weights, 16 * 15)
            for kd in range(H):
                for kh in range(H):
                    last = nc.tensor.transpose(ps[:, PD, (kd * H + kh) * P:(kd * H + kh + 1) * P],
                                               wl[:, kh, kd * P:(kd + 1) * P], ident[:, :])
            last.then_inc(s_wtr, 1)
            pe.wait_ge(s_x, 16)
            pe.wait_ge(s_rec, CHUNKS)


            def pq_step(q, par):
                if live(q, BLOCKS):
                    pe.wait_ge(s_xin, q + 1)
                    if later(q, 2):
                        pe.wait_ge(s_xtev, q - 1)
                    for h in range(H):
                        last = nc.tensor.transpose(ps[:, PZ + par, h * P:h * P + NB],
                                                   xin[:, par, h * P:(h + 1) * P], ident[0:NB, 0:NB])
                    last.then_inc(s_xt, 1)
                if live(q - 1, BLOCKS):
                    o = 1 - par
                    pe.wait_ge(s_xtev, q)
                    if later(q - 1, 2):
                        pe.wait_ge(s_pqrow, q - 2)
                    for h in range(H):
                        last = nc.tensor.matmul(ps[0:NB, PM + o, :], col[:, o, h, 0:NB], w1[:, h:2 * H:H, :],
                                                start=h == 0, stop=h == H - 1)
                    last.then_inc(s_pqmm, 1)
            steps(pe, BLOCKS, 1, pq_step)

            for l in range(2):
                s = e[l]

                def keys(q, par):
                    pe.wait_ge(s["staged"], q + 1)
                    if later(q, 1):
                        pe.wait_ge(s["same"], q)
                    for u in range(QT):
                        last = nc.tensor.transpose(ps[:, PK, u * P:(u + 1) * P],
                                                   key[:, par, u, 0:1].to_broadcast([P, P]), ident[:, :])
                    last.then_inc(s["keyt"], 1)

                def sum_same(q, par):
                    pe.wait_ge(s["same"], q + 1)
                    if l == 0:
                        pe.wait_ge(s["msg"], q + 1)
                        if later(q, 1):
                            pe.wait_ge(s["tot"], q)
                        for u in range(QT):
                            last = nc.tensor.matmul(ps[:, PD + u // 2, u % 2 * D:(u % 2 + 1) * D],
                                                    same[:, par, u, :], msg[:, par, u, 0:D], start=True, stop=True)
                    else:
                        pe.wait_ge(s[f"gat{par}"], half_count(q) * (16 * QT))
                        if later(q, 1):
                            pe.wait_ge(s["tot"], q)
                            pe.wait_ge(s["totv"], q)
                        for u in range(QT):
                            last = nc.tensor.matmul(ps[:, PM + u, 0:CW], same[:, par, u, :], msg[:, par, u, :],
                                                    start=True, stop=True)
                    last.then_inc(s["ded"], 1)

                def norm_columns(q, par):
                    pe.wait_ge(s["norm"], q + 1)
                    if later(q, 1):
                        pe.wait_ge(s["zev"], 2 * q)
                    for h in range(H):
                        for u in range(QT):
                            last = nc.tensor.transpose(ps[:, PZ + h, u * P:(u + 1) * P],
                                                       act[:, par, u, h * P:(h + 1) * P], ident[:, :])
                    last.then_inc(s["ztr"], 1)

                def main(q, par):
                    pe.wait_ge(s["zev"], 2 * (q + 1))
                    if later(q, 1):
                        pe.wait_ge(s["msg"], q)
                    for u in range(QT):
                        to = ps[:, PM + u // 2, u % 2 * D:(u % 2 + 1) * D]
                        for h in range(H):
                            nc.tensor.matmul(to, zt[:, par, h, u * P:(u + 1) * P], w2[:, h, :],
                                             start=h == 0, stop=False)
                        last = nc.tensor.matmul(to, ones[:, :], b2r[:, :], start=False, stop=True)
                    last.then_inc(s["mm"], 1)

                if l == 0:
                    pe.wait_ge(s_bias, 6)

                    def step(q, par):
                        if live(q, QUADS):
                            keys(q, par)
                        if live(q - 2, QUADS):
                            sum_same(q - 2, par)
                        if live(q - 1, QUADS):
                            norm_columns(q - 1, 1 - par)
                            main(q - 1, 1 - par)
                    steps(pe, QUADS, 2, step)
                else:
                    pe.wait_ge(s_ones, 1)

                    def step(q, par):
                        keys(q, par)
                        sum_same(q, par)
                    steps(pe, QUADS, 0, step)

                t = k[l]
                if l == 0:
                    def columns(q, par):
                        pe.wait_ge(t["xin"], q + 1)
                        pe.wait_ge(t["agg"], q + 1)
                        if later(q, 2):
                            pe.wait_ge(t["colev"], q - 1)
                        for c in range(2 * H):
                            rows = (xin[:, par, c * P:(c + 1) * P] if c < H
                                    else agg[0:NB, par, (c - H) * P:(c - H + 1) * P])
                            last = nc.tensor.transpose(ps[:, PZ + par, c * P:c * P + NB], rows, ident[0:NB, 0:NB])
                        last.then_inc(t["cols"], 1)

                    def hidden(q, par):
                        pe.wait_ge(t["colev"], q + 1)
                        if later(q, 2):
                            pe.wait_ge(t["hpre"], q - 1)
                        for c in range(2 * H):
                            last = nc.tensor.matmul(ps[0:NB, PM + par, 0:D], col[:, par, c, 0:NB], u1[:, c, :],
                                                    start=c == 0, stop=c == 2 * H - 1)
                        last.then_inc(t["hmm"], 1)

                    def hidden_columns(q, par):
                        pe.wait_ge(t["hid"], q + 1)
                        if later(q, 2):
                            pe.wait_ge(t["hcolev"], q - 1)
                        for h in range(H):
                            last = nc.tensor.transpose(ps[:, PD + par, h * P:h * P + NB],
                                                       hid[0:NB, par, h * P:(h + 1) * P], ident[0:NB, 0:NB])
                        last.then_inc(t["hcols"], 1)

                    def update(q, par):
                        pe.wait_ge(t["hcolev"], q + 1)
                        if later(q, 2):
                            pe.wait_ge(t["oadd"], q - 1)
                        for h in range(H):
                            last = nc.tensor.matmul(ps[0:NB, PK + par, 0:D], hcol[:, par, h, 0:NB], u2[:, h, :],
                                                    start=h == 0, stop=h == H - 1)
                        last.then_inc(t["omm"], 1)

                    def step(q, par):
                        if live(q, BLOCKS):
                            columns(q, par)
                        if live(q - 1, BLOCKS):
                            hidden(q - 1, 1 - par)
                        if live(q - 2, BLOCKS):
                            hidden_columns(q - 2, par)
                        if live(q - 3, BLOCKS):
                            update(q - 3, 1 - par)
                    steps(pe, BLOCKS, 3, step)
                else:
                    def columns(q, par):
                        pe.wait_ge(t["agg"], q + 1)
                        if later(q, 2):
                            pe.wait_ge(t["colev"], q - 1)
                        for c in range(H):
                            last = nc.tensor.transpose(ps[:, PZ + par, c * P:c * P + NB],
                                                       agg[0:NB, par, c * P:(c + 1) * P], ident[0:NB, 0:NB])
                        last.then_inc(t["cols"], 1)

                    def project(q, par):
                        pe.wait_ge(t["colev"], q + 1)
                        if later(q, 2):
                            pe.wait_ge(t["oadd"], q - 1)
                        for c in range(H):
                            last = nc.tensor.matmul(ps[0:NB, PK + par, 0:D], col[:, par, c, 0:NB], wt[:, c, :],
                                                    start=c == 0, stop=c == H - 1)
                        last.then_inc(t["omm"], 1)

                    def step(q, par):
                        if live(q, BLOCKS):
                            columns(q, par)
                        if live(q - 1, BLOCKS):
                            project(q - 1, 1 - par)
                    steps(pe, BLOCKS, 1, step)

        @block.scalar
        def _(ac):
            ac.wait_ge(s_wtr, 1)
            nc.scalar.activation(flat(wt[:, :, :]), ps[:, PD, :], ACT.Copy).then_inc(s_wt, 1)
            ac.wait_ge(s_x, 16)

            def pq_step(q, par):
                if live(q, BLOCKS):
                    if later(q, 2):
                        ac.wait_ge(s_xt, q - 1)
                    nc.scalar.activation(xin[:, par, :], xs[:, bass.ds(q, 1), :].rearrange("p a d -> p (a d)"), ACT.Copy)\
                        .then_inc(s_xin, 1)
                if live(q - 1, BLOCKS):
                    o = 1 - par
                    ac.wait_ge(s_xt, q)
                    if later(q - 1, 2):
                        ac.wait_ge(s_pqmm, q - 2)
                    nc.scalar.activation(col[:, o, 0:H, 0:NB],
                                         ps[:, PZ + o, 0:H * P].rearrange("p (h n) -> p h n", h=H)[:, :, 0:NB],
                                         ACT.Copy).then_inc(s_xtev, 1)
            steps(ac, BLOCKS, 1, pq_step)

            for l in range(2):
                s = e[l]

                def silu(q, par):
                    ac.wait_ge(s["pre"], q + 1)
                    row = act[:, par, :, :].rearrange("p u d -> p (u d)")
                    nc.scalar.activation(row, row, ACT.Silu).then_inc(s["silu"], 1)

                def norm_columns(q, par):
                    ac.wait_ge(s["ztr"], q + 1)
                    if later(q, 2):
                        ac.wait_ge(s["mm"], q - 1)
                    for h in range(H):
                        nc.scalar.activation(zt[:, par, h, :], ps[:, PZ + h, :], ACT.Identity,
                                             bias=gb[:, h, 1:2], scale=gb[:, h, 0:1]).then_inc(s["zev"], 1)

                def message(q, par):
                    ac.wait_ge(s["mm"], q + 1)
                    if later(q, 2):
                        ac.wait_ge(s["ded"], q - 1)
                    nc.scalar.activation(msg[:, par, :, 0:D],
                                         ps[:, PM:PM + 2, :].rearrange("p b (u d) -> p (b u) d", u=2), ACT.Silu)\
                        .then_inc(s["msg"], 1)

                def total(q, par):
                    ac.wait_ge(s["ded"], q + 1)
                    if later(q, 2):
                        ac.wait_ge(s["added"], (q - 1) * (16 * QT))
                    if l == 0:
                        nc.scalar.activation(tot[:, par, :, 0:D],
                                             ps[:, PD:PD + 2, :].rearrange("p b (u d) -> p (b u) d", u=2), ACT.Copy)\
                            .then_inc(s["tot"], 1)
                    else:
                        nc.scalar.activation(tot[:, par, 0:2, :], ps[:, PM:PM + 2, 0:CW], ACT.Copy).then_inc(s["tot"], 1)

                if l == 0:
                    ac.wait_ge(s_weights, 16 * 15)

                    def step(q, par):
                        if live(q, QUADS):
                            silu(q, par)
                        if live(q - 2, QUADS):
                            total(q - 2, par)
                        if live(q - 1, QUADS):
                            norm_columns(q - 1, 1 - par)
                            message(q - 1, 1 - par)
                    steps(ac, QUADS, 2, step)
                else:
                    steps(ac, QUADS, 0, total)

                t = k[l]
                if l == 0:
                    def step(q, par):
                        if live(q, BLOCKS):
                            if later(q, 2):
                                ac.wait_ge(t["cols"], q - 1)
                            nc.scalar.activation(xin[:, par, :], xs[:, bass.ds(q, 1), :].rearrange("p a d -> p (a d)"),
                                                 ACT.Copy).then_inc(t["xin"], 1)
                        if live(q - 1, BLOCKS):
                            o = 1 - par
                            ac.wait_ge(t["cols"], q)
                            if later(q - 1, 2):
                                ac.wait_ge(t["hmm"], q - 2)
                            nc.scalar.activation(col[:, o, :, 0:NB],
                                                 ps[:, PZ + o, :].rearrange("p (h n) -> p h n", n=P)[:, :, 0:NB],
                                                 ACT.Copy).then_inc(t["colev"], 1)
                        if live(q - 2, BLOCKS):
                            ac.wait_ge(t["hpre"], q - 1)
                            if later(q - 2, 2):
                                ac.wait_ge(t["hcols"], q - 3)
                            nc.scalar.activation(hid[0:NB, par, :], hpre[0:NB, par, :], ACT.Silu).then_inc(t["hid"], 1)
                        if live(q - 3, BLOCKS):
                            o = 1 - par
                            ac.wait_ge(t["hcols"], q - 2)
                            if later(q - 3, 2):
                                ac.wait_ge(t["omm"], q - 4)
                            nc.scalar.activation(hcol[:, o, :, 0:NB],
                                                 ps[:, PD + o, 0:H * P].rearrange("p (h n) -> p h n", n=P)[:, :, 0:NB],
                                                 ACT.Copy).then_inc(t["hcolev"], 1)
                    steps(ac, BLOCKS, 3, step)
                else:
                    def step(q, par):
                        ac.wait_ge(t["cols"], q + 1)
                        if later(q, 2):
                            ac.wait_ge(t["omm"], q - 1)
                        nc.scalar.activation(col[:, par, 0:H, 0:NB],
                                             ps[:, PZ + par, 0:H * P].rearrange("p (h n) -> p h n", n=P)[:, :, 0:NB],
                                             ACT.Copy).then_inc(t["colev"], 1)
                    steps(ac, BLOCKS, 0, step)

        @block.vector
        def _(dve):
            dve.wait_ge(s_edges, 16 * 9)
            nc.vector.tensor_copy(ends[:, :, :, :], loaded[:, 0:2].bitcast(i32)).then_inc(s_ends, 1)
            for c in range(CHUNKS):
                n = min(P, TILES - c * P)
                dve.wait_ge(s_etr, c + 1)
                at = slice(c * P, c * P + n)

                def got(a):
                    return ps[:, PZ + c % 2, a * P:a * P + n]
                nc.vector.tensor_scalar(rec[:, at, 0], got(0), 2.0, None, ALU.mult)
                nc.vector.tensor_scalar(rec[:, at, 1], got(1), 2.0, 1.0, ALU.mult, ALU.add)
                nc.vector.tensor_copy(rec[:, at, 2], got(0))
                nc.vector.tensor_copy(dstf[:, at], got(1))
                nc.vector.tensor_copy(rec[:, at, 3], got(2)).then_inc(s_rec, 1)
            dve.wait_ge(s_weights, 16 * 15)
            dve.wait_ge(s_const, 4)
            nc.vector.tensor_copy(b2p[:, 0, :], b2f[:, 0, :]).then_inc(s_bias, 1)
            for i in range(2):
                dve.wait_ge(s_bias, 2 * i + 1)
                nc.vector.tensor_tensor(b2f[:, i + 1, :], b2f[:, i, :], b2p[:, i, :], ALU.subtract).then_inc(s_bias, 1)
                dve.wait_ge(s_bias, 2 * i + 2)
                nc.vector.tensor_copy(b2p[:, i + 1, :], b2f[:, i + 1, :]).then_inc(s_bias, 1)
            dve.wait_ge(s_bias, 5)
            nc.vector.tensor_scalar(b2f[:, 0, :], b2p[:, 0, :], ident[:, 0:1], None, ALU.mult).then_inc(s_biasr, 1)
            dve.wait_ge(s_biasr, 1)
            nc.vector.scalar_tensor_tensor(out=b2f[:, 1, :], in0=b2p[:, 1, :], scalar=ident[:, 1:2], in1=b2f[:, 0, :],
                                           op0=ALU.mult, op1=ALU.add).then_inc(s_biasr, 1)
            dve.wait_ge(s_biasr, 2)
            nc.vector.scalar_tensor_tensor(out=b2r[:, :], in0=b2p[:, 2, :], scalar=ident[:, 2:3], in1=b2f[:, 1, :],
                                           op0=ALU.mult, op1=ALU.add).then_inc(s_bias, 1)

            def pq_step(q, par):
                dve.wait_ge(s_pqmm, q + 1)
                if later(q, 2):
                    dve.wait_ge(s_pqst[par], half_count(q - 2) * 16)
                nc.vector.tensor_tensor(msg[0:NB, par, 0:2, 0:D],
                                        ps[0:NB, PM + par, :].rearrange("p (a d) -> p a d", a=2),
                                        b1q[0:NB, :, :], ALU.add).then_inc(s_pqrow, 1)
            dve.wait_ge(s_zeroed, 2)
            steps(dve, BLOCKS, 0, pq_step)

            for l in range(2):
                s = e[l]

                def stage(q, par):
                    if later(q, 2):
                        dve.wait_ge(s[f"gat{par}"], half_count(q - 2) * (16 * QT * (2 - l)))
                        dve.wait_ge(s["keyt"], q - 1)
                        dve.wait_ge(s["sidx"], q - 1)
                    at = bass.ds(q * QT, QT)
                    if l == 0:
                        nc.vector.tensor_copy(idx[:, par, :, :], rec[:, at, 0:2])
                        nc.vector.tensor_copy(key[:, par, :, :], rec[:, at, 2:4]).then_inc(s["staged"], 1)
                    else:
                        nc.vector.tensor_copy(idx[:, par, :, 0], rec[:, at, 2])
                        nc.vector.tensor_copy(key[:, par, :, 0], dstf[:, at]).then_inc(s["staged"], 1)

                def pre(q, par):
                    dve.wait_ge(s[f"gat{par}"], half_count(q) * (32 * QT))
                    if later(q, 2):
                        dve.wait_ge(s["ztr"], q - 1)
                    for u in range(QT):
                        nc.vector.scalar_tensor_tensor(out=act[:, par, u, :], in0=w1c[:, :], scalar=key[:, par, u, 1:2],
                                                       in1=gat[:, par, u, 0, :], op0=ALU.mult, op1=ALU.add)\
                            .then_inc(s["prea"], 1)
                    dve.wait_ge(s["prea"], QT * (q + 1))
                    nc.vector.tensor_tensor(act[:, par, :, :], act[:, par, :, :], gat[:, par, :, 1, :], ALU.add)\
                        .then_inc(s["pre"], 1)

                def norm(q, par):
                    dve.wait_ge(s["silu"], q + 1)
                    for u in range(QT):
                        nc.vector.bn_stats(bst[:, par, u, :], act[:, par, u, :]).then_inc(s["bst"], 1)
                    dve.wait_ge(s["bst"], QT * (q + 1))
                    m = mom[:, par]
                    nc.vector.tensor_tensor(m[:, 0], bst[:, par, :, 1], bst[:, par, :, 4], ALU.subtract).then_inc(s["mom"], 1)
                    nc.vector.tensor_tensor(m[:, 1], bst[:, par, :, 1], bst[:, par, :, 4], ALU.add).then_inc(s["mom"], 1)
                    nc.vector.tensor_tensor(m[:, 2], bst[:, par, :, 2], bst[:, par, :, 5], ALU.add).then_inc(s["mom"], 1)
                    dve.wait_ge(s["mom"], 6 * q + 1)
                    nc.vector.scalar_tensor_tensor(out=m[:, 0], in0=m[:, 0], scalar=0.25, in1=m[:, 0],
                                                   op0=ALU.mult, op1=ALU.mult).then_inc(s["mom"], 1)
                    dve.wait_ge(s["mom"], 6 * q + 4)
                    nc.vector.scalar_tensor_tensor(out=m[:, 3], in0=m[:, 2], scalar=1.0 / D, in1=m[:, 0],
                                                   op0=ALU.mult, op1=ALU.add).then_inc(s["mom"], 1)
                    nc.vector.tensor_scalar(m[:, 4], m[:, 1], 0.5, None, ALU.mult).then_inc(s["mom"], 1)
                    dve.wait_ge(s["mom"], 6 * q + 6)
                    inverse_root(dve, m[:, 3], [nwt[:, par, i] for i in range(5)], s["newt"], q * NEWTON_OPS)
                    dve.wait_ge(s["newt"], (q + 1) * NEWTON_OPS)
                    for u in range(QT):
                        last = nc.vector.tensor_scalar(act[:, par, u, :], act[:, par, u, :], m[:, 4, u:u + 1],
                                                       nwt[:, par, 4, u:u + 1], ALU.subtract, ALU.mult)
                    last.then_inc(s["norm"], 1)

                def find_same(q, par):
                    dve.wait_ge(s["keyt"], q + 1)
                    if later(q, 2):
                        dve.wait_ge(s["ded"], q - 1)
                        dve.wait_ge(s["added"], (q - 1) * (16 * QT))
                    nc.vector.tensor_tensor(same[:, par, :, :], ps[:, PK, :].rearrange("p (u n) -> p u n", u=QT),
                                            key[:, par, :, 0:1].to_broadcast([P, QT, P]), ALU.is_equal)\
                        .then_inc(s["same"], 1)
                    dve.wait_ge(s["same"], q + 1)
                    if later(q, 1):
                        dve.wait_ge(s["dup"], QT * q)
                    for u in range(QT):
                        nc.vector.tensor_tensor_reduce(out=scr[:, u, :], in0=same[:, par, u, :], in1=lower[:, :],
                                                       scale=1.0, scalar=0.0, op0=ALU.mult, op1=ALU.add,
                                                       accum_out=dup[:, par, u:u + 1]).then_inc(s["dup"], 1)
                    nc.vector.tensor_tensor(dif[:, par, :, 0], trash[:, :], key[:, par, :, 0], ALU.subtract)\
                        .then_inc(s["dif"], 1)
                    dve.wait_ge(s["dup"], QT * (q + 1))
                    dve.wait_ge(s["dif"], 2 * q + 1)
                    nc.vector.scalar_tensor_tensor(out=dif[:, par, :, 1], in0=dup[:, par, :], scalar=0.5,
                                                   in1=dif[:, par, :, 0], op0=ALU.is_gt, op1=ALU.mult)\
                        .then_inc(s["dif"], 1)
                    dve.wait_ge(s["dif"], 2 * q + 2)
                    nc.vector.tensor_tensor(sidx[:, par, :], dif[:, par, :, 1], key[:, par, :, 0], ALU.add)\
                        .then_inc(s["sidx"], 1)

                def total(q, par):
                    dve.wait_ge(s["ded"], q + 1)
                    if later(q, 2):
                        dve.wait_ge(s["added"], (q - 1) * (16 * QT))
                    nc.vector.tensor_copy(tot[:, par, 2:4, :], ps[:, PM + 2:PM + 4, 0:CW]).then_inc(s["totv"], 1)

                if l == 0:
                    dve.wait_ge(s_rec, CHUNKS)
                    nc.vector.memset(agg[:, :, :], 0.0).then_inc(s["totv"], QUADS)
                    stage(0, 0)

                    def step(q, par):
                        if live(q + 1, QUADS):
                            stage(q + 1, 1 - par)
                        if live(q, QUADS):
                            pre(q, par)
                        if live(q - 1, QUADS):
                            norm(q - 1, 1 - par)
                        if live(q, QUADS):
                            find_same(q, par)
                    steps(dve, QUADS, 1, step, ahead=1)
                else:
                    for c, v in ((0, 1.0), (1, 0.0)):
                        at = slice(D, D + 1) if c == 0 else slice(D + 1, CW)
                        nc.vector.memset(msg[:, :, :, at], v).then_inc(s_ones, 1)
                    stage(0, 0)

                    def step(q, par):
                        if live(q + 1, QUADS):
                            stage(q + 1, 1 - par)
                        if live(q, QUADS):
                            find_same(q, par)
                        if live(q - 1, QUADS):
                            total(q - 1, 1 - par)
                    steps(dve, QUADS, 1, step, ahead=1)

                t = k[l]
                width = D if l == 0 else CW

                def add_tables(q, par):
                    dve.wait_ge(t[f"load{par}"], half_count(q) * (16 * TABLES))
                    nc.vector.tensor_tensor(half[0:NB, par, :, 0:width], blk[0:NB, par, 0:2, 0:width],
                                            blk[0:NB, par, 2:4, 0:width], ALU.add).then_inc(t["half"], 1)
                    dve.wait_ge(t["half"], q + 1)
                    if later(q, 2):
                        dve.wait_ge(t["cols"], q - 1)
                    if l == 0:
                        nc.vector.tensor_tensor(agg[0:NB, par, 0:D], half[0:NB, par, 0, 0:D], half[0:NB, par, 1, 0:D],
                                                ALU.add).then_inc(t["agg"], 1)
                    else:
                        nc.vector.tensor_tensor(agg[0:NB, par, :], half[0:NB, par, 0, :], half[0:NB, par, 1, :],
                                                ALU.add).then_inc(t["cnt"], 1)
                        dve.wait_ge(t["cnt"], 3 * q + 1)
                        nc.vector.tensor_scalar(cnt[0:NB, par, 0:1], agg[0:NB, par, D:D + 1], 1.0, None, ALU.max)\
                            .then_inc(t["cnt"], 1)
                        dve.wait_ge(t["cnt"], 3 * q + 2)
                        nc.vector.reciprocal(cnt[0:NB, par, 1:2], cnt[0:NB, par, 0:1]).then_inc(t["cnt"], 1)
                        dve.wait_ge(t["cnt"], 3 * q + 3)
                        nc.vector.tensor_scalar(agg[0:NB, par, 0:D], agg[0:NB, par, 0:D], cnt[0:NB, par, 1:2], None,
                                                ALU.mult).then_inc(t["agg"], 1)

                def hidden(q, par):
                    dve.wait_ge(t["hmm"], q + 1)
                    if later(q, 2):
                        dve.wait_ge(t["hid"], q - 1)
                    nc.vector.tensor_tensor(hpre[0:NB, par, :], ps[0:NB, PM + par, 0:D], ub1b[0:NB, :], ALU.add)\
                        .then_inc(t["hpre"], 1)

                def result(q, par):
                    dve.wait_ge(t["omm"], q + 1)
                    row = xs[:, bass.ds(q, 1), :].rearrange("p a d -> p (a d)")
                    nc.vector.tensor_tensor(hpre2[0:NB, par, :], ps[0:NB, PK + par, 0:D],
                                            (ub2b if l == 0 else blb)[0:NB, :], ALU.add).then_inc(t["oadd"], 1)
                    dve.wait_ge(t["oadd"], q + 1)
                    if l == 0:
                        nc.vector.scalar_tensor_tensor(out=row, in0=row, scalar=2.0, in1=hpre2[0:NB, par, :],
                                                       op0=ALU.mult, op1=ALU.add).then_inc(t["res"], 1)
                    else:
                        nc.vector.scalar_tensor_tensor(out=row, in0=hpre2[0:NB, par, :], scalar=0.0, in1=row,
                                                       op0=ALU.max, op1=ALU.add).then_inc(t["res"], 1)
                    dve.wait_ge(t["res"], q + 1)
                    dve.sem_inc(s_dturn, 1)
                    nc.vector.bn_stats(bst2[:, par, :], row).then_inc(t["bst"], 1)
                    dve.wait_ge(t["bst"], q + 1)
                    dve.sem_inc(s_dturn, 1)
                    nc.vector.bn_aggr(mv2[:, par, :], bst2[:, par, :]).then_inc(t["aggr"], 1)
                    dve.wait_ge(t["aggr"], q + 1)
                    nc.vector.tensor_copy(mst[:, bass.ds(q, 1), :].rearrange("p a d -> p (a d)"), mv2[:, par, :])\
                        .then_inc(t["stat"], 1)

                if l == 0:
                    def step(q, par):
                        if live(q, BLOCKS):
                            add_tables(q, par)
                        if live(q - 1, BLOCKS):
                            hidden(q - 1, 1 - par)
                        if live(q - 3, BLOCKS):
                            result(q - 3, 1 - par)
                    steps(dve, BLOCKS, 3, step)
                else:
                    def step(q, par):
                        if live(q, BLOCKS):
                            add_tables(q, par)
                        if live(q - 1, BLOCKS):
                            result(q - 1, 1 - par)
                    steps(dve, BLOCKS, 1, step)
                dve.wait_ge(t["stat"], BLOCKS)
                inverse_root(dve, mst[:, :, 1], [nwb[:, i] for i in range(5)], t["newt"], 0)
                dve.wait_ge(t["newt"], NEWTON_OPS)

                def normalise(q, par):
                    row = xs[:, bass.ds(q, 1), :].rearrange("p a d -> p (a d)")
                    nc.vector.tensor_scalar(row, row, mst[:, bass.ds(q, 1), 0], nwb[:, 4, bass.ds(q, 1)],
                                            ALU.subtract, ALU.mult).then_inc(t["norm"], 1)
                steps(dve, BLOCKS, 0, normalise)
                dve.wait_ge(t["norm"], BLOCKS)
                nc.vector.memset(cnt[:, 0, 0:1], 0.0).then_inc(s_done[l], 1)


_INS = ["x", "src", "dst", "edge_weight1", "L0_gnn_mW1", "L0_gnn_mb1", "L0_gnn_ln_g", "L0_gnn_ln_b", "L0_gnn_mW2",
        "L0_gnn_mb2", "L0_gnn_uW1", "L0_gnn_ub1", "L0_gnn_uW2", "L0_gnn_ub2", "L1_gnn_W", "L1_gnn_b"]


def kernel(**inputs):
    import numpy as _np
    import concourse.bacc as _bacc
    from concourse import mybir as _mybir
    from concourse.bass_utils import run_bass_kernel_spmd as _run

    nc = _bacc.Bacc("TRN2", target_bir_lowering=False, num_devices=1)
    arrays, args = {}, []
    for name in _INS:
        a = _np.ascontiguousarray(inputs[name])
        arrays[f"in_{name}_dram"] = a
        args.append(nc.dram_tensor(f"in_{name}_dram", a.shape, _mybir.dt.from_np(a.dtype), kind="ExternalInput").ap())
    args.append(nc.dram_tensor("out_0_dram", (N, D), _mybir.dt.float32, kind="ExternalOutput").ap())
    gnn(nc, *args)
    r = _run(nc, [arrays], core_ids=[0])
    return r.results[0]["out_0_dram"]
```

```python
import concourse.bass as bass
from concourse import mybir
from contextlib import ExitStack

N = 6250
D = 256
E = 106250
P = 128
H = D // P
LN_EPS = 1e-5

QT = 4
TILES = -(-E // P)
CHUNKS = -(-TILES // P)
FULL = E // P
REST = E - FULL * P
NB = 125
BLOCKS = N // NB
QUADS = -(-(TILES + BLOCKS - 1) // QT)
VISITS = QUADS * QT
ROWS = N + NB
PAD = N
SUMROWS = 50 * P
TABLES = QT
PARTS = 3
CW = D + 1
ROUND = 1.5 * 2.0 ** 23
MAGIC = 0x5F3759DF
NEWTON = 3
NEWTON_OPS = 4 + 3 * NEWTON
assert BLOCKS * NB == N and SUMROWS >= N + P and REST > 0 and NB + PARTS == P and D == 256


def gnn(nc, x, src, dst, edge_w, mW1, mb1, ln_g, ln_b, mW2, mb2, uW1, ub1, uW2, ub2, W, b, out):
    f32, i32, bf16 = mybir.dt.float32, mybir.dt.int32, mybir.dt.bfloat16
    ALU = mybir.AluOpType
    ACT = mybir.ActivationFunctionType
    AX = mybir.AxisListType

    p_tab = nc.dram_tensor("p_tab", (ROWS, D), f32, kind="Internal").ap()
    rec_tab = nc.dram_tensor("rec_tab", (CHUNKS * P * P, 3), f32, kind="Internal").ap()
    x1_tab = nc.dram_tensor("x1_tab", (ROWS, D), f32, kind="Internal").ap()
    sums = [nc.dram_tensor(f"sum_{r}", (SUMROWS, D), f32, kind="Internal").ap() for r in range(TABLES)]

    with ExitStack() as ctx:
        def sb(name, shape, dt=f32):
            return ctx.enter_context(nc.sbuf_tensor(name, shape, dt))

        def sem(name):
            return ctx.enter_context(nc.semaphore(name))

        ident = sb("ident", [P, P])
        identh = sb("identh", [P, P], bf16)
        lower = sb("lower", [P, P])
        nextp = sb("nextp", [P, P])
        wrap = sb("wrap", [P, P])
        zeros = sb("zeros", [P, D])
        ones = sb("ones", [P, P], bf16)
        onesf = sb("onesf", [P, P])
        nodes = sb("nodes", [P, NB], bf16)
        w1 = sb("w1", [P, 2 * H, D])
        w2 = sb("w2", [P, H, D])
        u1 = sb("u1", [P, 2 * H, D])
        u2 = sb("u2", [P, H, D])
        wl = sb("wl", [P, H, D])
        wt = sb("wt", [P, H, D])
        b1b = sb("b1b", [P, D])
        b2r = sb("b2r", [P, D], bf16)
        ub1b = sb("ub1b", [P, D])
        ub2b = sb("ub2b", [P, D])
        blb = sb("blb", [P, D])
        gb = sb("gb", [P, H, 2])
        big = sb("big", [P, BLOCKS, PARTS, D], bf16)
        rows = big[:, :, :, :].rearrange("p j k d -> p (j k d)").bitcast(f32)\
            .rearrange("p (j c) -> p j c", j=BLOCKS)
        vsrc = sb("vsrc", [P, VISITS], i32)
        vkey = sb("vkey", [P, VISITS])
        vkeyh = sb("vkeyh", [P, 2, VISITS], bf16)
        vloc = sb("vloc", [P, VISITS])
        vwgt = sb("vwgt", [P, VISITS, PARTS], bf16)
        vblk = sb("vblk", [P, VISITS], i32)
        trash_i = sb("trash_i", [P, QT], i32)
        trash = sb("trash", [P, QT])
        mst = sb("mst", [NB, BLOCKS, 2])
        nwb = sb("nwb", [NB, 5, BLOCKS])

        work = sb("work", [P, 12544])
        at_ = [0]

        def cut(shape, dt=f32, parts=P):
            n = 1
            for m in shape:
                n *= m
            words = n if dt != bf16 else n // 2
            ap = work[:, at_[0]:at_[0] + words]
            at_[0] += words
            assert at_[0] <= 12544, at_[0]
            ap = ap if dt == f32 else ap.bitcast(dt)
            names = "abcd"[:len(shape)]
            ap = ap.rearrange(f"p ({' '.join(names)}) -> p {' '.join(names)}", **dict(zip(names, shape)))
            return ap[0:parts]

        gat = cut([2, QT, D])
        act = cut([2, QT, D])
        zt = cut([2, H, QT * P])
        msg = cut([2, QT, CW + 3])
        tot = cut([2, QT, D])
        same = cut([2, QT, P])
        hot = cut([2, QT, P], bf16)
        hott = cut([2, QT, P], bf16)
        assert at_[0] <= 12544
        at_[0] = 0
        loaded = cut([3, CHUNKS, P])
        ends = cut([2, CHUNKS, P])
        pick = cut([2, 2, VISITS])
        vdst = cut([VISITS])
        wrest = cut([2, VISITS])
        viota = cut([VISITS])
        at_[0] = 0
        blk = cut([2, TABLES, D])
        half = cut([2, 2, D])
        agg = cut([2, D])
        col = cut([2, 2 * H, P])
        xin = cut([2, D])
        hpre = cut([2, D])
        hpre2 = cut([2, D])
        hid = cut([2, D])
        hcol = cut([2, H, P])
        pcol = sb("pcol", [P, 2, H, P])
        pxin = sb("pxin", [NB, 2, D])
        prow = sb("prow", [NB, 2, D])
        qres = sb("qres", [NB, 2, D])
        w1cf = sb("w1cf", [P, 2, D])
        w1cp = sb("w1cp", [P, PARTS, D], bf16)
        b2f = sb("b2f", [P, 3, D])
        b2p = sb("b2p", [P, PARTS, D], bf16)

        scr = sb("scr", [P, QT, P])
        idx = sb("idx", [P, 2, QT], i32)
        key = sb("key", [P, 2, QT])
        keyh = sb("keyh", [P, 2, 2, QT], bf16)
        dup = sb("dup", [P, 2, QT])
        dif = sb("dif", [P, 2, QT, 2])
        sidx = sb("sidx", [P, 2, QT], i32)
        bst = sb("bst", [P, 2, QT, 6])
        mom = sb("mom", [P, 2, 5, QT])
        nwt = sb("nwt", [P, 2, 5, QT])
        cnt = sb("cnt", [P, 2, 2])
        mv2 = sb("mv2", [NB, 2, 2])
        bst2 = sb("bst2", [NB, 2, 6])
        tnum_i = sb("tnum_i", [P, CHUNKS], i32)
        viota_i = sb("viota_i", [P, VISITS], i32)
        tnum = sb("tnum", [P, CHUNKS])
        thi = sb("thi", [P, 4, CHUNKS])
        tprev = sb("tprev", [P, CHUNKS])
        first_v = sb("first_v", [P, CHUNKS])
        next_v = sb("next_v", [P, CHUNKS])
        down = sb("down", [P, CHUNKS + 1])
        down_i = sb("down_i", [P, 1], i32)

        scratch = big[:, :, :, :].rearrange("p j k d -> p (j k d)").bitcast(f32)
        W_ALL = CHUNKS * P
        f_blk, f_mask, f_pos, f_cum0, f_cum1 = (scratch[:, i * W_ALL:(i + 1) * W_ALL] for i in range(5))
        f_cum = (f_cum0, f_cum1)
        f_pos_i = scratch[:, 5 * W_ALL:6 * W_ALL].bitcast(i32)
        f_rec = scratch[:, 6 * W_ALL:9 * W_ALL].rearrange("p (c a) -> p c a", a=3)
        f_sorted = scratch[:, 9 * W_ALL:12 * W_ALL]
        f_run = sb("f_run", [P, 2])
        f_slot_i = sb("f_slot_i", [P, 1], i32)
        f_slot = sb("f_slot", [P, 3])

        ps = ctx.enter_context(nc.psum_tensor("ps", [P, 7, 512], f32))
        psh = ctx.enter_context(nc.psum_tensor("psh", [P, QT, P], bf16))
        PM, PZ, PP, PK = 0, 2, 4, 6

        def flat(ap):
            return ap.rearrange("p a b -> p (a b)")

        SPLIT = ((0, 112), (112, NB))

        s_const, s_constc, s_zeroed, s_pad = sem("s_const"), sem("s_constc"), sem("s_zeroed"), sem("s_pad")
        s_edges, s_weights, s_tables = sem("s_edges"), sem("s_weights"), sem("s_tables")
        s_ends, s_tile, s_prev, s_range = sem("s_ends"), sem("s_tile"), sem("s_prev"), sem("s_range")
        s_done_g, s_count, s_blk, s_pick, s_picked, s_visit = (sem("s_done_g"), sem("s_count"), sem("s_blk"),
                                                               sem("s_pick"), sem("s_picked"), sem("s_visit"))
        s_bias, s_wpart, s_wrow, s_wtr, s_wt = sem("s_bias"), sem("s_wpart"), sem("s_wrow"), sem("s_wtr"), sem("s_wt")
        s_xload = [sem("s_xload0"), sem("s_xload1")]
        s_xt, s_xtev, s_pqmm, s_prow, s_q1, s_qr, s_q2, s_q3 = (
            sem("s_xt"), sem("s_xtev"), sem("s_pqmm"), sem("s_prow"), sem("s_q1"), sem("s_qr"), sem("s_q2"), sem("s_q3"))
        s_pst = [sem("s_pst0"), sem("s_pst1")]
        s_turn_pool, s_turn_dve, s_turn_act = sem("s_turn_pool"), sem("s_turn_dve"), sem("s_turn_act")
        s_down, s_flag, f_ends, f_tile, f_prev, f_range = (sem("s_down"), sem("s_flag"), sem("f_ends"), sem("f_tile"),
                                                           sem("f_prev"), sem("f_range"))
        f_seq, f_count, f_based, f_ready, f_copied, f_done, f_load, f_back = (
            sem("f_seq"), sem("f_count"), sem("f_based"), sem("f_ready"), sem("f_copied"), sem("f_done"), sem("f_load"),
            sem("f_back"))
        s_x1st, s_out, s_ones = sem("s_x1st"), sem("s_out"), sem("s_ones")

        EDGE = [["staged", "gat0", "gat1", "hot", "hott", "hev", "keyt", "same", "dup", "dif", "sidx", "qexp", "pre",
                 "keys", "silu", "bst", "mom", "newt", "norm", "ztr", "zev", "mm", "msg", "ded", "tot", "added"],
                ["staged", "gat0", "gat1", "hot", "agg", "acc"]]
        e = [{n: sem(f"e{l}_{n}") for n in EDGE[l]} for l in range(2)]
        BLOCK = ["load0", "load1", "xcopy", "half", "agg", "cnt", "cols", "colev", "hmm", "hpre", "hid", "hcols", "hcolev",
                 "omm", "oadd", "res", "bst", "aggr", "stat", "newt", "norm"]
        k = [{n: sem(f"b{l}_{n}") for n in BLOCK} for l in range(2)]

        block = ctx.enter_context(nc.Block())

        def steps(eng, n, lag, step, ahead=0):
            lo = 4
            hi = (n - ahead) // 2 * 2
            for q in range(-ahead, lo):
                step(q, q % 2)
            with eng.Fori(lo // 2, hi // 2) as it:
                for par in (0, 1):
                    step(it * 2 + par, par)
            for q in range(hi, n + lag):
                step(q, q % 2)

        def live(q, n):
            return not isinstance(q, int) or 0 <= q < n

        def half_count(q):
            return q // 2 + 1

        def later(q, n):
            return not isinstance(q, int) or q >= n

        def inverse_root(dve, v, w, sem_, at, between=()):
            nc.vector.tensor_scalar(w[0], v, LN_EPS, None, ALU.add).then_inc(sem_, 1)
            nc.vector.tensor_scalar(w[1], v, LN_EPS, -0.5, ALU.add, ALU.mult).then_inc(sem_, 1)
            dve.wait_ge(sem_, at + 1)
            nc.vector.tensor_scalar(w[2].bitcast(i32), w[0].bitcast(i32), 1, None, ALU.logical_shift_right)\
                .then_inc(sem_, 1)
            dve.wait_ge(sem_, at + 3)
            nc.vector.tensor_scalar(w[4].bitcast(i32), w[2].bitcast(i32), -1.0, float(MAGIC), ALU.mult, ALU.add)\
                .then_inc(sem_, 1)
            for i in range(NEWTON):
                dve.wait_ge(sem_, at + 4 + 3 * i)
                nc.vector.tensor_tensor(w[2], w[4], w[4], ALU.mult).then_inc(sem_, 1)
                if i < len(between):
                    between[i]()
                dve.wait_ge(sem_, at + 5 + 3 * i)
                nc.vector.tensor_tensor(w[3], w[2], w[1], ALU.mult).then_inc(sem_, 1)
                dve.wait_ge(sem_, at + 6 + 3 * i)
                nc.vector.scalar_tensor_tensor(out=w[4], in0=w[3], scalar=1.5, in1=w[4], op0=ALU.add, op1=ALU.mult)\
                    .then_inc(sem_, 1)

        def tiles_down(eng):
            eng.wait_ge(s_flag, 1)
            return eng.value_load(down_i[0:1, 0:1], min_val=0, max_val=TILES)

        @block.sync
        def _(sp):
            sp.wait_ge(s_pad, 3)
            last, left = CHUNKS - 1, FULL - (CHUNKS - 1) * P
            for a, arr in enumerate((src, dst, edge_w.rearrange("e o -> (e o)"))):
                dest = loaded[:, a] if a == 2 else loaded[:, a].bitcast(i32)
                sp.dma_start(dest[:, 0:last, :], arr[0:last * P * P].rearrange("(k r e) -> r k e", r=P, e=P))\
                    .then_inc(s_edges, 16)
                sp.dma_start(dest[0:left, last, :], arr[last * P * P:FULL * P].rearrange("(r e) -> r e", e=P))\
                    .then_inc(s_edges, 16)
                sp.dma_start(dest[left:left + 1, last, 0:REST], arr[FULL * P:E].rearrange("(r e) -> r e", e=REST))\
                    .then_inc(s_edges, 16)
            for dest, arr in ((w1, mW1[0:2 * D, :]), (w2, mW2), (u1, uW1), (u2, uW2), (wl, W)):
                sp.dma_start(dest[:, :, :], arr.rearrange("(k p) d -> p k d", p=P)).then_inc(s_weights, 16)
            for dest, row in ((w1cf[:, 0, :], mW1[2 * D:2 * D + 1, :]), (b1b[:, :], mb1), (b2f[:, 0, :], mb2),
                              (ub1b[:, :], ub1), (ub2b[:, :], ub2), (blb[:, :], b)):
                row = row if len(row.shape) == 2 else row.rearrange("(a n) -> a n", a=1)
                sp.dma_start(dest, row.to_broadcast([P, D])).then_inc(s_weights, 16)
            for a, row in enumerate((ln_g, ln_b)):
                for h in range(H):
                    sp.dma_start(gb[:, h, a:a + 1], row[h * P:(h + 1) * P].rearrange("(p a) -> p a", a=1))\
                        .then_inc(s_weights, 16)
            sp.wait_ge(s_zeroed, 1)
            for t in sums:
                sp.dma_start(t.rearrange("(p a) d -> p a d", p=P),
                             zeros[:, :].unsqueeze(1).to_broadcast([P, SUMROWS // P, D])).then_inc(s_tables, 16)
            for t in (p_tab, x1_tab):
                sp.dma_start(t[N:ROWS, :], zeros[0:NB, :]).then_inc(s_tables, 16)
            with sp.If(tiles_down(sp) > 0):
                sp.wait_ge(f_done, 16 * W_ALL)
                sp.dma_start(f_sorted.rearrange("p (k e) -> p k e", k=CHUNKS),
                             rec_tab.rearrange("(k r e) a -> r k (e a)", r=P, e=P)).then_inc(f_load, 16)
            sp.wait_ge(s_wpart, 5)
            sp.dma_start(big[NB:P, :, :, :].rearrange("p j k d -> p j (k d)"),
                         w1cp[0:PARTS, :, :].rearrange("p k d -> p (k d)").unsqueeze(1)
                         .to_broadcast([PARTS, BLOCKS, PARTS * D])).then_inc(s_wrow, 16)

            def pq_step(q, par):
                if live(q + 1, BLOCKS):
                    o = 1 - par
                    if later(q + 1, 2):
                        sp.wait_ge(s_xt, q)
                    for a, z in SPLIT:
                        sp.dma_start(pxin[a:z, o, :], x[bass.ds((q + 1) * NB + a, z - a), :]).then_inc(s_xload[o], 16)
                if live(q - 1, BLOCKS):
                    o = 1 - par
                    sp.wait_ge(s_prow, q)
                    for a, z in SPLIT:
                        sp.dma_start(p_tab[bass.ds((q - 1) * NB + a, z - a), :], prow[a:z, o, :])\
                            .then_inc(s_pst[o], 16)
            steps(sp, BLOCKS, 1, pq_step, ahead=1)

            sp.wait_ge(e[0]["added"], 16 * QT * QUADS)

            def load_0(q, par):
                if later(q, 2):
                    sp.wait_ge(k[0]["half"], q - 1)
                for r in range(TABLES):
                    for a, z in SPLIT:
                        sp.dma_start(blk[a:z, par, r, :], sums[r][bass.ds(q * NB + a, z - a), :])\
                            .then_inc(k[0][f"load{par}"], 16)
                for a, z in SPLIT:
                    sp.dma_start(rows[a:z, bass.ds(q, 1), 0:D].rearrange("p a d -> p (a d)"),
                                 x[bass.ds(q * NB + a, z - a), :]).then_inc(k[0][f"load{par}"], 16)
            steps(sp, BLOCKS, 0, load_0)

            def store(l, to):
                def step(q, par):
                    sp.wait_ge(k[l]["norm"], q + 1)
                    for a, z in SPLIT:
                        sp.dma_start(to[bass.ds(q * NB + a, z - a), :],
                                     rows[a:z, bass.ds(q, 1), 0:D].rearrange("p a d -> p (a d)"))\
                            .then_inc(s_x1st if l == 0 else s_out, 16)
                return step
            steps(sp, BLOCKS, 0, store(0, x1_tab))

            sp.wait_ge(e[1]["acc"], QUADS * QT)

            def load_1(q, par):
                if later(q, 2):
                    sp.wait_ge(k[1]["res"], q - 1)
                for a, z in SPLIT:
                    sp.dma_start(xin[a:z, par, :], x1_tab[bass.ds(q * NB + a, z - a), :])\
                        .then_inc(k[1][f"load{par}"], 16)
            steps(sp, BLOCKS, 0, load_1)
            steps(sp, BLOCKS, 0, store(1, out))
            sp.wait_ge(s_out, 32 * BLOCKS)

        @block.gpsimd
        def _(pool):
            nc.gpsimd.memset(loaded[:, 0:2, CHUNKS - 1, :].bitcast(i32), PAD).then_inc(s_pad, 2)
            nc.gpsimd.memset(loaded[:, 2, CHUNKS - 1, :], 0.0).then_inc(s_pad, 1)
            nc.gpsimd.memset(zeros[:, :], 0.0).then_inc(s_zeroed, 1)
            nc.gpsimd.memset(ident[:, :], 0.0).then_inc(s_constc, 1)
            nc.gpsimd.memset(lower[:, :], 1.0).then_inc(s_constc, 1)
            nc.gpsimd.memset(nextp[:, :], 0.0).then_inc(s_constc, 1)
            nc.gpsimd.memset(wrap[:, :], 0.0).then_inc(s_constc, 1)
            nc.gpsimd.memset(ones[:, :], 1.0).then_inc(s_const, 1)
            nc.gpsimd.memset(onesf[:, :], 1.0).then_inc(s_const, 1)
            nc.gpsimd.iota(trash_i[:, :], pattern=[[0, QT]], base=N, channel_multiplier=1).then_inc(s_constc, 1)
            nc.gpsimd.iota(tnum_i[:, :], pattern=[[P, CHUNKS]], base=0, channel_multiplier=1).then_inc(s_constc, 1)
            nc.gpsimd.iota(viota_i[:, :], pattern=[[1, VISITS]], base=0, channel_multiplier=0).then_inc(s_constc, 1)
            pool.wait_ge(s_constc, 7)
            for mat, op, fill, base in ((ident, ALU.not_equal, 1.0, 0), (lower, ALU.is_gt, 0.0, 0),
                                        (nextp, ALU.not_equal, 1.0, 1)):
                nc.gpsimd.affine_select(out=mat[:, :], in_=mat[:, :], compare_op=op, fill=fill, base=base,
                                        pattern=[[-1, P]], channel_multiplier=1).then_inc(s_const, 1)
            nc.gpsimd.affine_select(out=wrap[:, :], in_=wrap[:, :], compare_op=ALU.not_equal, fill=1.0, base=1 - P,
                                    pattern=[[P, P]], channel_multiplier=1).then_inc(s_const, 1)
            nc.gpsimd.tensor_copy(trash[:, :], trash_i[:, :]).then_inc(s_const, 1)
            nc.gpsimd.tensor_copy(tnum[:, :], tnum_i[:, :]).then_inc(s_const, 1)
            pool.wait_ge(s_const, 8)
            nc.gpsimd.tensor_copy(identh[:, :], ident[:, :]).then_inc(s_const, 1)
            nc.gpsimd.tensor_copy(nodes[:, :], viota_i[:, 0:NB]).then_inc(s_const, 1)
            with pool.If(tiles_down(pool) > 0):
                pool.wait_ge(f_ready, 5)

                def place(c):
                    nc.gpsimd.tensor_copy(f_slot_i[:, :], f_pos_i[:, bass.ds(c, 1)]).then_inc(f_copied, 1)
                    nc.gpsimd.tensor_copy(f_slot[:, :], f_rec[:, bass.ds(c, 1), :].rearrange("p a d -> p (a d)"))\
                        .then_inc(f_copied, 1)
                    pool.wait_ge(f_copied, 2 * (c + 1))
                    pool.sem_inc(s_turn_pool, 1)
                    pool.indirect_dma_start(
                        out=rec_tab[:, :], out_offset=bass.IndirectOffsetOnAxis(ap=f_slot_i[:, 0:1], axis=0),
                        in_=f_slot[:, :], in_offset=None).then_inc(f_done, 16)
                place(0)
                with pool.Fori(1, W_ALL) as c:
                    pool.wait_ge(f_done, 16 * c)
                    pool.sem_inc(s_turn_pool, 1)
                    place(c)
            pool.wait_ge(s_tables, 16 * (TABLES + 2))
            for par in (0, 1):
                pool.wait_ge(s_pst[par], 32 * BLOCKS // 2)

            def gather(l, table, slots):
                def step(q, par):
                    pool.wait_ge(e[l]["staged"], q + 1)
                    if l == 0 and later(q, 2):
                        pool.wait_ge(e[l]["pre"], q - 1)
                    for u in range(QT):
                        if l == 1 and later(q, 2):
                            pool.wait_ge(e[l]["agg"], (q - 2) * QT + u + 1)
                        if u == 0 or (l == 1 and later(q, 2)):
                            pool.sem_inc(s_turn_pool, 1)
                        pool.indirect_dma_start(
                            out=slots[:, par, u, 0:D], out_offset=None, in_=table[:, :],
                            in_offset=bass.IndirectOffsetOnAxis(ap=idx[:, par, u:u + 1], axis=0))\
                            .then_inc(e[l][f"gat{par}"], 16)
                return step

            def add(q, par):
                pool.wait_ge(e[0]["tot"], q + 1)
                pool.wait_ge(e[0]["sidx"], q + 1)
                if later(q, 1):
                    pool.wait_ge(e[0]["added"], q * (16 * QT))
                pool.sem_inc(s_turn_pool, 1)
                for u in range(QT):
                    pool.indirect_dma_start(
                        out=sums[u][:, :], in_=tot[:, par, u, :], in_offset=None,
                        out_offset=bass.IndirectOffsetOnAxis(ap=sidx[:, par, u:u + 1], axis=0),
                        compute_op=ALU.add).then_inc(e[0]["added"], 16)

            gather_0 = gather(0, p_tab, gat)

            def step_0(q, par):
                if live(q + 1, QUADS):
                    gather_0(q + 1, 1 - par)
                if live(q - 2, QUADS):
                    add(q - 2, par)
            steps(pool, QUADS, 2, step_0, ahead=1)

            def copy_x(q, par):
                pool.wait_ge(k[0][f"load{par}"], half_count(q) * (32 * (TABLES + 1)))
                if later(q, 2):
                    pool.wait_ge(k[0]["cols"], q - 1)
                pool.sem_inc(s_turn_pool, 1)
                nc.gpsimd.tensor_copy(xin[0:NB, par, :], rows[0:NB, bass.ds(q, 1), 0:D]
                                      .rearrange("p a d -> p (a d)")).then_inc(k[0]["xcopy"], 1)
            steps(pool, BLOCKS, 0, copy_x)
            pool.wait_ge(s_x1st, 32 * BLOCKS)
            pool.wait_ge(s_tables, 16 * (TABLES + 2))
            steps(pool, QUADS, 0, gather(1, x1_tab, msg))

        @block.tensor
        def _(pe):
            pe.wait_ge(s_const, 10)
            pe.wait_ge(s_weights, 16 * 15)
            for kd in range(H):
                for kh in range(H):
                    last = nc.tensor.transpose(ps[:, PK, (kd * H + kh) * P:(kd * H + kh + 1) * P],
                                               wl[:, kh, kd * P:(kd + 1) * P], ident[:, :])
            last.then_inc(s_wtr, 1)
            pe.wait_ge(s_wt, 1)
            def tile_before(tile, prev):
                pe.wait_ge(tile, 4)
                nc.tensor.matmul(ps[:, PK, 0:CHUNKS], nextp[:, :], thi[:, 3, :], start=True, stop=False)
                nc.tensor.matmul(ps[:, PK, 1:CHUNKS], wrap[:, :], thi[:, 3, 0:CHUNKS - 1], start=False, stop=True)\
                    .then_inc(prev, 1)
            tile_before(s_tile, s_prev)
            pe.wait_ge(s_down, 2)
            nc.tensor.matmul(ps[:, PP, 0:1], onesf[:, :], down[:, CHUNKS:CHUNKS + 1], start=True, stop=True)\
                .then_inc(s_down, 1)
            with pe.If(tiles_down(pe) > 0):
                def counts(q):
                    pe.wait_ge(f_count, q + 1)
                    nc.tensor.matmul(ps[:, PZ, 0:1], lower[:, :], f_cum[0][:, W_ALL - 1:W_ALL], start=True, stop=True)
                    nc.tensor.matmul(ps[:, PZ, 1:2], onesf[:, :], f_cum[0][:, W_ALL - 1:W_ALL], start=True, stop=True)\
                        .then_inc(f_based, 1)
                with pe.Fori(0, BLOCKS + 1) as q:
                    counts(q)
                tile_before(f_tile, f_prev)
            HV = VISITS // 2
            for c in range(CHUNKS):
                pe.wait_ge(s_done_g, c + 1)
                for v in range(2):
                    last = nc.tensor.matmul(ps[:, v, 0:HV], onesf[:, :], pick[:, c % 2, 0, v * HV:(v + 1) * HV],
                                            start=c == 0, stop=c == CHUNKS - 1)
                last.then_inc(s_count, 1)
            pe.wait_ge(s_blk, 1)
            pe.wait_ge(s_edges, 16 * 9)
            for c in range(CHUNKS):
                pe.wait_ge(s_pick, 2 * (c + 1))
                for a in range(3):
                    edges = ends[:, a, c, :] if a < 2 else loaded[:, 2, c, :]
                    for v in range(2):
                        last = nc.tensor.matmul(ps[:, 2 * a + v, 0:HV], edges, pick[:, c % 2, 0, v * HV:(v + 1) * HV],
                                                start=c == 0, stop=c == CHUNKS - 1)
                last.then_inc(s_picked, 1)
            pe.wait_ge(s_visit, 4)

            def pq_step(q, par):
                if live(q, BLOCKS):
                    pe.wait_ge(s_xload[par], half_count(q) * 32)
                    if later(q, 2):
                        pe.wait_ge(s_xtev, q - 1)
                    for h in range(H):
                        last = nc.tensor.transpose(ps[:, PZ + par, h * P:h * P + NB],
                                                   pxin[:, par, h * P:(h + 1) * P], ident[0:NB, 0:NB])
                    last.then_inc(s_xt, 1)
                if live(q - 1, BLOCKS):
                    o = 1 - par
                    pe.wait_ge(s_xtev, q)
                    if later(q - 1, 2):
                        pe.wait_ge(s_qr, q - 2)
                    for h in range(H):
                        last = nc.tensor.matmul(ps[0:NB, PM + o, :], pcol[:, o, h, 0:NB], w1[:, h:2 * H:H, :],
                                                start=h == 0, stop=h == H - 1)
                    last.then_inc(s_pqmm, 1)
            steps(pe, BLOCKS, 1, pq_step)

            s = e[0]

            def hot_columns(q, par):
                pe.wait_ge(s["hot"], q + 1)
                if later(q, 1):
                    pe.wait_ge(s["hev"], q)
                for u in range(QT):
                    last = nc.tensor.transpose(psh[:, u, :], hot[:, par, u, :], identh[:, :])
                last.then_inc(s["hott"], 1)

            def keys(q, par):
                pe.wait_ge(s["keys"], q + 1)
                if later(q, 1):
                    pe.wait_ge(s["same"], q)
                for u in range(QT):
                    for i in range(2):
                        last = nc.tensor.matmul(ps[:, PK, u * P:(u + 1) * P],
                                                keyh[:, par, i, u:u + 1].to_broadcast([P, P]), identh[:, :],
                                                start=i == 0, stop=i == 1)
                last.then_inc(s["keyt"], 1)

            def sum_same(q, par):
                pe.wait_ge(s["same"], q + 1)
                pe.wait_ge(s["msg"], q + 1)
                for u in range(QT):
                    last = nc.tensor.matmul(ps[:, PM + u // 2, u % 2 * D:(u % 2 + 1) * D],
                                            same[:, par, u, :], msg[:, par, u, 0:D], start=True, stop=True)
                last.then_inc(s["ded"], 1)

            def norm_columns(q, par):
                pe.wait_ge(s["norm"], q + 1)
                if later(q, 1):
                    pe.wait_ge(s["zev"], 2 * q)
                for h in range(H):
                    for u in range(QT):
                        last = nc.tensor.transpose(ps[:, PZ + h, u * P:(u + 1) * P],
                                                   act[:, par, u, h * P:(h + 1) * P], ident[:, :])
                    last.then_inc(s["ztr"], 1)

            def visit_blocks(q):
                return [pe.value_load(vblk[0:1, bass.ds(q * QT + u, 1)], min_val=0, max_val=BLOCKS - 1)
                        for u in range(QT)]

            def expand(q, par, blocks_):
                pe.wait_ge(s["hev"], q + 1)
                if later(q, 1):
                    pe.wait_ge(s["pre"], q)
                for u in range(QT):
                    for i in range(PARTS):
                        last = nc.tensor.matmul(ps[:, PP + u // 2, u % 2 * D:(u % 2 + 1) * D], hott[:, par, u, :],
                                                big[:, bass.ds(blocks_[u], 1), i, :].rearrange("p a d -> p (a d)"),
                                                start=i == 0, stop=i == PARTS - 1)
                last.then_inc(s["qexp"], 1)

            def main(q, par):
                pe.wait_ge(s["zev"], 2 * (q + 1))
                if later(q, 1):
                    pe.wait_ge(s["tot"], q)
                for u in range(QT):
                    to = ps[:, PM + u // 2, u % 2 * D:(u % 2 + 1) * D]
                    for h in range(H):
                        nc.tensor.matmul(to, zt[:, par, h, u * P:(u + 1) * P], w2[:, h, :], start=h == 0, stop=False)
                    last = nc.tensor.matmul(to, ones[:, :], b2r[:, :], start=False, stop=True)
                last.then_inc(s["mm"], 1)

            def step_0(q, par):
                if live(q + 1, QUADS):
                    of = visit_blocks(q + 1)
                if live(q - 1, QUADS):
                    norm_columns(q - 1, 1 - par)
                if live(q - 2, QUADS):
                    sum_same(q - 2, par)
                if live(q + 1, QUADS):
                    expand(q + 1, 1 - par, of)
                if live(q, QUADS):
                    keys(q, par)
                if live(q - 1, QUADS):
                    main(q - 1, 1 - par)
                if live(q + 2, QUADS):
                    hot_columns(q + 2, par)
            pe.wait_ge(s_bias, 6)
            pe.wait_ge(s_wrow, 16)
            pe.wait_ge(s_q3, BLOCKS)
            steps(pe, QUADS, 2, step_0, ahead=2)

            t = k[0]

            def columns(q, par):
                pe.wait_ge(t["xcopy"], q + 1)
                pe.wait_ge(t["agg"], q + 1)
                if later(q, 2):
                    pe.wait_ge(t["colev"], q - 1)
                for c in range(2 * H):
                    part = (xin[0:NB, par, c * P:(c + 1) * P] if c < H
                            else agg[0:NB, par, (c - H) * P:(c - H + 1) * P])
                    last = nc.tensor.transpose(ps[:, PZ + par, c * P:c * P + NB], part, ident[0:NB, 0:NB])
                last.then_inc(t["cols"], 1)

            def hidden(q, par):
                pe.wait_ge(t["colev"], q + 1)
                if later(q, 2):
                    pe.wait_ge(t["hpre"], q - 1)
                for c in range(2 * H):
                    last = nc.tensor.matmul(ps[0:NB, PM + par, 0:D], col[:, par, c, 0:NB], u1[:, c, :],
                                            start=c == 0, stop=c == 2 * H - 1)
                last.then_inc(t["hmm"], 1)

            def hidden_columns(q, par):
                pe.wait_ge(t["hid"], q + 1)
                if later(q, 2):
                    pe.wait_ge(t["hcolev"], q - 1)
                for h in range(H):
                    last = nc.tensor.transpose(ps[:, PP + par, h * P:h * P + NB],
                                               hid[0:NB, par, h * P:(h + 1) * P], ident[0:NB, 0:NB])
                last.then_inc(t["hcols"], 1)

            def update(q, par):
                pe.wait_ge(t["hcolev"], q + 1)
                if later(q, 1):
                    pe.wait_ge(t["oadd"], q)
                for h in range(H):
                    last = nc.tensor.matmul(ps[0:NB, PK, par * D:(par + 1) * D], hcol[:, par, h, 0:NB], u2[:, h, :],
                                            start=h == 0, stop=h == H - 1)
                last.then_inc(t["omm"], 1)

            def block_0(q, par):
                if live(q, BLOCKS):
                    columns(q, par)
                if live(q - 1, BLOCKS):
                    hidden(q - 1, 1 - par)
                if live(q - 2, BLOCKS):
                    hidden_columns(q - 2, par)
                if live(q - 3, BLOCKS):
                    update(q - 3, 1 - par)
            steps(pe, BLOCKS, 3, block_0)

            def aggregate(q, par):
                pe.wait_ge(e[1]["hot"], q + 1)
                pe.wait_ge(e[1][f"gat{par}"], half_count(q) * (16 * QT))
                for u in range(QT):
                    if later(q, 1):
                        pe.wait_ge(e[1]["acc"], (q - 1) * QT + u + 1)
                    nc.tensor.matmul(ps[0:NB, u, 0:CW], same[:, par, u, 0:NB], msg[:, par, u, 0:CW],
                                     start=True, stop=True).then_inc(e[1]["agg"], 1)
            pe.wait_ge(s_ones, 1)
            steps(pe, QUADS, 0, aggregate)

            t = k[1]

            def columns_1(q, par):
                pe.wait_ge(t["agg"], q + 1)
                if later(q, 2):
                    pe.wait_ge(t["colev"], q - 1)
                for c in range(H):
                    last = nc.tensor.transpose(ps[:, PZ + par, c * P:c * P + NB],
                                               agg[0:NB, par, c * P:(c + 1) * P], ident[0:NB, 0:NB])
                last.then_inc(t["cols"], 1)

            def project(q, par):
                pe.wait_ge(t["colev"], q + 1)
                if later(q, 1):
                    pe.wait_ge(t["oadd"], q)
                for c in range(H):
                    last = nc.tensor.matmul(ps[0:NB, PK, par * D:(par + 1) * D], col[:, par, c, 0:NB], wt[:, c, :],
                                            start=c == 0, stop=c == H - 1)
                last.then_inc(t["omm"], 1)

            def block_1(q, par):
                if live(q, BLOCKS):
                    columns_1(q, par)
                if live(q - 1, BLOCKS):
                    project(q - 1, 1 - par)
            steps(pe, BLOCKS, 1, block_1)

        @block.scalar
        def _(ac):
            ac.wait_ge(s_wtr, 1)
            nc.scalar.activation(flat(wt[:, :, :]), ps[:, PK, :], ACT.Copy).then_inc(s_wt, 1)

            def pq_step(q, par):
                if live(q, BLOCKS):
                    ac.wait_ge(s_xt, q + 1)
                    if later(q, 2):
                        ac.wait_ge(s_pqmm, q - 1)
                    nc.scalar.activation(pcol[:, par, :, 0:NB],
                                         ps[:, PZ + par, 0:H * P].rearrange("p (h n) -> p h n", h=H)[:, :, 0:NB],
                                         ACT.Copy).then_inc(s_xtev, 1)
                if live(q - 1, BLOCKS):
                    ac.wait_ge(s_prow, q)
                    ac.sem_inc(s_turn_act, 1)
                    nc.scalar.activation(big[0:NB, bass.ds(q - 1, 1), 0, :].rearrange("p a d -> p (a d)"),
                                         ps[0:NB, PM + 1 - par, D:2 * D], ACT.Copy).then_inc(s_q1, 1)
                if live(q - 2, BLOCKS):
                    ac.wait_ge(s_qr, q - 1)
                    ac.sem_inc(s_turn_act, 1)
                    nc.scalar.activation(big[0:NB, bass.ds(q - 2, 1), 1, :].rearrange("p a d -> p (a d)"),
                                         qres[:, par, :], ACT.Copy).then_inc(s_q2, 1)
            steps(ac, BLOCKS, 2, pq_step)

            s = e[0]

            def hot_columns(q, par):
                ac.wait_ge(s["hott"], q + 1)
                if later(q, 2):
                    ac.wait_ge(s["qexp"], q - 1)
                nc.scalar.activation(hott[:, par, :, :], psh[:, :, :], ACT.Copy).then_inc(s["hev"], 1)

            def silu(q, par):
                ac.wait_ge(s["pre"], q + 1)
                nc.scalar.activation(act[:, par, :, :], act[:, par, :, :], ACT.Silu).then_inc(s["silu"], 1)

            def norm_columns(q, par, h):
                ac.wait_ge(s["ztr"], 2 * q + h + 1)
                if h == 0 and later(q, 2):
                    ac.wait_ge(s["mm"], q - 1)
                nc.scalar.activation(zt[:, par, h, :], ps[:, PZ + h, :], ACT.Identity,
                                     bias=gb[:, h, 1:2], scale=gb[:, h, 0:1]).then_inc(s["zev"], 1)

            def message(q, par):
                ac.wait_ge(s["mm"], q + 1)
                if later(q, 2):
                    ac.wait_ge(s["ded"], q - 1)
                nc.scalar.activation(msg[:, par, :, 0:D],
                                     ps[:, PM:PM + 2, :].rearrange("p b (u d) -> p (b u) d", u=2), ACT.Silu)\
                    .then_inc(s["msg"], 1)

            def total(q, par):
                ac.wait_ge(s["ded"], q + 1)
                if later(q, 2):
                    ac.wait_ge(s["added"], (q - 1) * (16 * QT))
                nc.scalar.activation(tot[:, par, :, :],
                                     ps[:, PM:PM + 2, :].rearrange("p b (u d) -> p (b u) d", u=2), ACT.Copy)\
                    .then_inc(s["tot"], 1)

            def step_0(q, par):
                if live(q - 1, QUADS):
                    norm_columns(q - 1, 1 - par, 0)
                if live(q, QUADS):
                    silu(q, par)
                if live(q - 1, QUADS):
                    norm_columns(q - 1, 1 - par, 1)
                if live(q - 2, QUADS):
                    total(q - 2, par)
                if live(q - 1, QUADS):
                    message(q - 1, 1 - par)
                if live(q + 2, QUADS):
                    hot_columns(q + 2, par)
            ac.wait_ge(s_weights, 16 * 15)
            steps(ac, QUADS, 2, step_0, ahead=2)

            t = k[0]

            def block_0(q, par):
                if live(q, BLOCKS):
                    ac.wait_ge(t["cols"], q + 1)
                    if later(q, 2):
                        ac.wait_ge(t["hmm"], q - 1)
                    nc.scalar.activation(col[:, par, :, 0:NB],
                                         ps[:, PZ + par, :].rearrange("p (h n) -> p h n", n=P)[:, :, 0:NB],
                                         ACT.Copy).then_inc(t["colev"], 1)
                if live(q - 1, BLOCKS):
                    o = 1 - par
                    ac.wait_ge(t["hpre"], q)
                    if later(q - 1, 2):
                        ac.wait_ge(t["hcols"], q - 2)
                    nc.scalar.activation(hid[0:NB, o, :], hpre[0:NB, o, :], ACT.Silu).then_inc(t["hid"], 1)
                if live(q - 2, BLOCKS):
                    ac.wait_ge(t["hcols"], q - 1)
                    if later(q - 2, 2):
                        ac.wait_ge(t["omm"], q - 3)
                    nc.scalar.activation(hcol[:, par, :, 0:NB],
                                         ps[:, PP + par, 0:H * P].rearrange("p (h n) -> p h n", n=P)[:, :, 0:NB],
                                         ACT.Copy).then_inc(t["hcolev"], 1)
            steps(ac, BLOCKS, 2, block_0)

            t = k[1]

            def block_1(q, par):
                ac.wait_ge(t["cols"], q + 1)
                if later(q, 2):
                    ac.wait_ge(t["omm"], q - 1)
                nc.scalar.activation(col[:, par, 0:H, 0:NB],
                                     ps[:, PZ + par, 0:H * P].rearrange("p (h n) -> p h n", n=P)[:, :, 0:NB],
                                     ACT.Copy).then_inc(t["colev"], 1)
            steps(ac, BLOCKS, 0, block_1)

        @block.vector
        def _(dve):
            def split(first, rest, parts, sem_, at):
                left = [first, *rest]
                nc.vector.tensor_copy(parts[0], first).then_inc(sem_, 1)
                for i in range(PARTS - 1):
                    dve.wait_ge(sem_, at + 2 * i + 1)
                    nc.vector.tensor_tensor(left[i + 1], left[i], parts[i], ALU.subtract).then_inc(sem_, 1)
                    dve.wait_ge(sem_, at + 2 * i + 2)
                    nc.vector.tensor_copy(parts[i + 1], left[i + 1]).then_inc(sem_, 1)

            dve.wait_ge(s_edges, 16 * 9)
            nc.vector.tensor_copy(ends[:, :, :, :], loaded[:, 0:2].bitcast(i32)).then_inc(s_ends, 1)
            dve.wait_ge(s_ends, 1)
            dve.wait_ge(s_const, 10)

            def find_ranges(sems_, at):
                ends_, tile, prev, range_ = sems_
                nc.vector.tensor_reduce(out=thi[:, 0, :], in_=ends[:, 1], axis=AX.X, op=ALU.min).then_inc(tile, 1)
                nc.vector.tensor_reduce(out=thi[:, 1, :], in_=ends[:, 1], axis=AX.X, op=ALU.max).then_inc(tile, 1)
                dve.wait_ge(tile, 2)
                nc.vector.tensor_scalar(thi[:, 0:2, :], thi[:, 0:2, :], 1.0 / NB, (NB - 1) / (2.0 * NB),
                                        ALU.mult, ALU.subtract).then_inc(tile, 1)
                dve.wait_ge(tile, 3)
                nc.vector.tensor_scalar(thi[:, 0:2, :], thi[:, 0:2, :], ROUND, None, ALU.add).then_inc(ends_, 1)
                dve.wait_ge(ends_, at + 1)
                nc.vector.tensor_scalar(thi[:, 2:4, :], thi[:, 0:2, :], ROUND, float(BLOCKS - 1), ALU.subtract, ALU.min)\
                    .then_inc(tile, 1)
                dve.wait_ge(tile, 4)
                nc.vector.scalar_tensor_tensor(out=next_v[:, :], in0=thi[:, 3, :], scalar=1.0, in1=tnum[:, :],
                                               op0=ALU.add, op1=ALU.add).then_inc(range_, 1)
                dve.wait_ge(prev, 1)
                nc.vector.tensor_tensor(first_v[:, :], ps[:, PK, 0:CHUNKS], tnum[:, :], ALU.add).then_inc(range_, 1)
                dve.wait_ge(range_, 2)

            nc.vector.tensor_copy(viota[:, :], viota_i[:, :]).then_inc(s_ends, 1)
            find_ranges((s_ends, s_tile, s_prev, s_range), 2)
            nc.vector.tensor_tensor(down[:, 0:CHUNKS], ps[:, PK, 0:CHUNKS], thi[:, 2, :], ALU.is_gt).then_inc(s_down, 1)
            dve.wait_ge(s_down, 1)
            nc.vector.tensor_reduce(out=down[:, CHUNKS:CHUNKS + 1], in_=down[:, 0:CHUNKS], axis=AX.X, op=ALU.add)\
                .then_inc(s_down, 1)
            dve.wait_ge(s_down, 3)
            nc.vector.tensor_copy(down_i[:, :], ps[:, PP, 0:1]).then_inc(s_flag, 1)
            with dve.If(tiles_down(dve) > 0):
                flat_dst = ends[:, 1].rearrange("p k e -> p (k e)")
                nc.vector.tensor_scalar(f_blk, flat_dst, 1.0 / NB, (NB - 1) / (2.0 * NB), ALU.mult, ALU.subtract)\
                    .then_inc(f_back, 1)
                dve.wait_ge(f_back, 1)
                nc.vector.tensor_scalar(f_blk, f_blk, ROUND, None, ALU.add).then_inc(f_back, 1)
                dve.wait_ge(f_back, 2)
                nc.vector.tensor_scalar(f_blk, f_blk, ROUND, None, ALU.subtract).then_inc(f_back, 1)
                nc.vector.memset(f_run[:, :], 0.0).then_inc(f_back, 1)
                nc.vector.memset(f_pos, 0.0).then_inc(f_back, 1)
                for a, whole in enumerate((ends[:, 0], ends[:, 1], loaded[:, 2])):
                    nc.vector.tensor_copy(f_rec[:, :, a], whole.rearrange("p k e -> p (k e)")).then_inc(f_ready, 1)
                dve.wait_ge(f_back, 5)
                shifts = [1 << i for i in range(W_ALL.bit_length())]
                assert len(shifts) % 2 == 0 and shifts[-1] < W_ALL
                SEQ = 1 + 2 * len(shifts) + 5

                def block_places(q):
                    n = [0]

                    def then(instruction):
                        instruction.then_inc(f_seq, 1)
                        n[0] += 1
                        dve.wait_ge(f_seq, q * SEQ + n[0])
                    then(nc.vector.tensor_scalar(f_mask, f_blk, viota[:, bass.ds(q, 1)], None, ALU.is_equal))
                    for i, d in enumerate(shifts):
                        fr, to = f_mask if i == 0 else f_cum[i % 2], f_cum[(i + 1) % 2]
                        then(nc.vector.tensor_copy(to[:, 0:d], fr[:, 0:d]))
                        then(nc.vector.tensor_tensor(to[:, d:], fr[:, d:], fr[:, 0:W_ALL - d], ALU.add))
                    dve.sem_inc(f_count, 1)
                    dve.wait_ge(f_based, q + 1)
                    then(nc.vector.scalar_tensor_tensor(out=f_run[:, 1:2], in0=ps[:, PZ, 0:1], scalar=-1.0,
                                                        in1=f_run[:, 0:1], op0=ALU.add, op1=ALU.add))
                    then(nc.vector.tensor_tensor(f_run[:, 0:1], ps[:, PZ, 1:2], f_run[:, 0:1], ALU.add))
                    then(nc.vector.tensor_scalar(f_cum[1], f_cum[0], f_run[:, 1:2], None, ALU.add))
                    then(nc.vector.tensor_tensor(f_cum[0], f_cum[1], f_mask, ALU.mult))
                    then(nc.vector.tensor_tensor(f_pos, f_pos, f_cum[0], ALU.add))
                with dve.Fori(0, BLOCKS + 1) as q:
                    block_places(q)
                nc.vector.tensor_copy(f_pos_i, f_pos).then_inc(f_ready, 1)
                dve.wait_ge(f_ready, 4)
                dve.sem_inc(f_ready, 1)
                dve.wait_ge(f_load, 16)
                for a, whole in enumerate((ends[:, 0], ends[:, 1], loaded[:, 2])):
                    nc.vector.tensor_copy(whole.rearrange("p k e -> p (k e)"),
                                          f_sorted.rearrange("p (c a) -> p c a", a=3)[:, :, a]).then_inc(f_ends, 1)
                dve.wait_ge(f_ends, 3)
                find_ranges((f_ends, f_tile, f_prev, f_range), 3)
            HV = VISITS // 2
            for c in range(CHUNKS):
                if c >= 2:
                    dve.wait_ge(s_count, c - 1)
                nc.vector.tensor_scalar(pick[:, c % 2, 0, :], viota[:, :], next_v[:, c:c + 1], None, ALU.is_ge)\
                    .then_inc(s_done_g, 1)
            dve.wait_ge(s_count, CHUNKS)
            nc.vector.tensor_tensor(vdst[:, :].rearrange("p (a v) -> p a v", a=2),
                                    viota[:, :].rearrange("p (a v) -> p a v", a=2), ps[:, 0:2, 0:HV], ALU.subtract)\
                .then_inc(s_blk, 1)
            for c in range(CHUNKS):
                if c >= 2:
                    dve.wait_ge(s_picked, c - 1)
                nc.vector.tensor_scalar(pick[:, c % 2, 1, :], viota[:, :], next_v[:, c:c + 1], None, ALU.is_ge)\
                    .then_inc(s_pick, 1)
                dve.wait_ge(s_pick, 2 * c + 1)
                nc.vector.scalar_tensor_tensor(out=pick[:, c % 2, 0, :], in0=viota[:, :], scalar=first_v[:, c:c + 1],
                                               in1=pick[:, c % 2, 1, :], op0=ALU.is_ge, op1=ALU.subtract)\
                    .then_inc(s_pick, 1)
            dve.wait_ge(s_blk, 1)
            nc.vector.tensor_copy(vblk[:, :], vdst[:, :]).then_inc(s_blk, 1)
            dve.wait_ge(s_picked, CHUNKS)

            def picked(a):
                return ps[:, 2 * a:2 * a + 2, 0:HV]

            def halves(ap):
                return ap.rearrange("p (a v) -> p a v", a=2)
            nc.vector.tensor_copy(halves(vsrc[:, :]), picked(0)).then_inc(s_visit, 1)
            nc.vector.tensor_copy(halves(vkey[:, :]), picked(0)).then_inc(s_visit, 1)
            nc.vector.scalar_tensor_tensor(out=halves(vloc[:, :]), in0=halves(vdst[:, :]), scalar=float(-NB),
                                           in1=picked(1), op0=ALU.mult, op1=ALU.add).then_inc(s_visit, 1)
            nc.vector.tensor_copy(halves(wrest[:, 0, :]), picked(2)).then_inc(s_visit, 1)
            dve.wait_ge(s_visit, 4)
            nc.vector.tensor_scalar(pick[:, 0, 0, :], vloc[:, :], 0.0, None, ALU.is_ge).then_inc(s_visit, 1)
            dve.wait_ge(s_visit, 5)
            nc.vector.scalar_tensor_tensor(out=pick[:, 0, 1, :], in0=vloc[:, :], scalar=float(NB), in1=pick[:, 0, 0, :],
                                           op0=ALU.is_lt, op1=ALU.mult).then_inc(s_visit, 1)
            dve.wait_ge(s_visit, 6)
            nc.vector.scalar_tensor_tensor(out=pick[:, 1, 0, :], in0=vkey[:, :], scalar=float(-PAD),
                                           in1=pick[:, 0, 1, :], op0=ALU.add, op1=ALU.mult).then_inc(s_visit, 1)
            dve.wait_ge(s_visit, 7)
            nc.vector.tensor_scalar(vkey[:, :], pick[:, 1, 0, :], float(PAD), None, ALU.add).then_inc(s_visit, 1)
            dve.wait_ge(s_visit, 8)
            nc.vector.tensor_copy(vkeyh[:, 0, :], vkey[:, :]).then_inc(s_visit, 1)
            dve.wait_ge(s_visit, 9)
            nc.vector.tensor_tensor(vkeyh[:, 1, :], vkey[:, :], vkeyh[:, 0, :], ALU.subtract).then_inc(s_visit, 1)
            split(wrest[:, 0, :], [wrest[:, 1, :], viota[:, :]], [vwgt[:, :, i] for i in range(PARTS)], s_visit, 10)
            dve.wait_ge(s_visit, 10 + 2 * PARTS - 1)
            dve.wait_ge(s_weights, 16 * 15)
            split(w1cf[:, 0, :], [w1cf[:, 1, :], w1cf[:, 0, :]], [w1cp[:, i, :] for i in range(PARTS)], s_wpart, 0)
            split(b2f[:, 0, :], [b2f[:, 1, :], b2f[:, 2, :]], [b2p[:, i, :] for i in range(PARTS)], s_bias, 0)
            dve.wait_ge(s_bias, 5)
            nc.vector.tensor_scalar(b2f[:, 0, :], b2p[:, 0, :], ident[:, 0:1], None, ALU.mult).then_inc(s_range, 1)
            dve.wait_ge(s_range, 3)
            nc.vector.scalar_tensor_tensor(out=b2f[:, 1, :], in0=b2p[:, 1, :], scalar=ident[:, 1:2], in1=b2f[:, 0, :],
                                           op0=ALU.mult, op1=ALU.add).then_inc(s_range, 1)
            dve.wait_ge(s_range, 4)
            nc.vector.scalar_tensor_tensor(out=b2r[:, :], in0=b2p[:, 2, :], scalar=ident[:, 2:3], in1=b2f[:, 1, :],
                                           op0=ALU.mult, op1=ALU.add).then_inc(s_bias, 1)

            def pq_step(q, par):
                if live(q, BLOCKS):
                    dve.wait_ge(s_pqmm, q + 1)
                    if later(q, 2):
                        dve.wait_ge(s_pst[par], half_count(q - 2) * 32)
                        dve.wait_ge(s_q3, q - 1)
                    nc.vector.tensor_tensor(prow[:, par, :], ps[0:NB, PM + par, 0:D], b1b[0:NB, :], ALU.add)\
                        .then_inc(s_prow, 1)
                    dve.wait_ge(s_q1, q + 1)
                    nc.vector.tensor_tensor(qres[:, par, :], ps[0:NB, PM + par, D:2 * D],
                                            big[0:NB, bass.ds(q, 1), 0, :].rearrange("p a d -> p (a d)"),
                                            ALU.subtract).then_inc(s_qr, 1)
                if live(q - 1, BLOCKS):
                    o = 1 - par
                    dve.wait_ge(s_q2, q)
                    nc.vector.tensor_tensor(big[0:NB, bass.ds(q - 1, 1), 2, :].rearrange("p a d -> p (a d)"),
                                            qres[:, o, :], big[0:NB, bass.ds(q - 1, 1), 1, :]
                                            .rearrange("p a d -> p (a d)"), ALU.subtract).then_inc(s_q3, 1)
            steps(dve, BLOCKS, 1, pq_step)

            s = e[0]

            def stage(q, par, l):
                if later(q, 2):
                    dve.wait_ge(e[l][f"gat{par}"], half_count(q - 2) * (16 * QT))
                    dve.sem_inc(s_turn_dve, 1)
                nc.vector.tensor_copy(idx[:, par, :], vsrc[:, bass.ds(q * QT, QT)]).then_inc(e[l]["staged"], 1)

            def stage_keys(q, par):
                if later(q, 2):
                    dve.wait_ge(s["keyt"], q - 1)
                    dve.wait_ge(s["sidx"], q - 1)
                    dve.sem_inc(s_turn_dve, 1)
                nc.vector.tensor_copy(key[:, par, :], vkey[:, bass.ds(q * QT, QT)])
                nc.vector.tensor_copy(keyh[:, par, :, :], vkeyh[:, :, bass.ds(q * QT, QT)]).then_inc(s["keys"], 1)

            def one_hot(q, par, u):
                if u == 0 and later(q, 2):
                    dve.wait_ge(s["hott"], q - 1)
                    dve.sem_inc(s_turn_dve, 1)
                if u < QT:
                    nc.vector.tensor_scalar(hot[:, par, u, 0:NB], nodes[:, :], vloc[:, bass.ds(q * QT + u, 1)], None,
                                            ALU.is_equal)
                else:
                    nc.vector.tensor_copy(hot[:, par, :, NB:P], vwgt[:, bass.ds(q * QT, QT), :]).then_inc(s["hot"], 1)

            def pre(q, par):
                dve.wait_ge(s[f"gat{par}"], half_count(q) * (16 * QT))
                dve.wait_ge(s["qexp"], q + 1)
                if later(q, 2):
                    dve.wait_ge(s["ztr"], 2 * (q - 1))
                nc.vector.tensor_tensor(act[:, par, :, :],
                                        ps[:, PP:PP + 2, :].rearrange("p b (u d) -> p (b u) d", u=2),
                                        gat[:, par, :, :], ALU.add).then_inc(s["pre"], 1)

            def norm(q, par):
                dve.wait_ge(s["silu"], q + 1)
                for u in range(QT):
                    nc.vector.bn_stats(bst[:, par, u, :], act[:, par, u, :]).then_inc(s["bst"], 1)
                more = live(q + 2, QUADS)
                if more:
                    one_hot(q + 2, par, 0)
                dve.wait_ge(s["bst"], QT * (q + 1))
                m = mom[:, par]
                nc.vector.tensor_tensor(m[:, 0], bst[:, par, :, 1], bst[:, par, :, 4], ALU.subtract).then_inc(s["mom"], 1)
                nc.vector.tensor_tensor(m[:, 1], bst[:, par, :, 1], bst[:, par, :, 4], ALU.add).then_inc(s["mom"], 1)
                nc.vector.tensor_tensor(m[:, 2], bst[:, par, :, 2], bst[:, par, :, 5], ALU.add).then_inc(s["mom"], 1)
                dve.wait_ge(s["mom"], 6 * q + 1)
                nc.vector.scalar_tensor_tensor(out=m[:, 0], in0=m[:, 0], scalar=0.25, in1=m[:, 0],
                                               op0=ALU.mult, op1=ALU.mult).then_inc(s["mom"], 1)
                if more:
                    one_hot(q + 2, par, 1)
                dve.wait_ge(s["mom"], 6 * q + 4)
                nc.vector.scalar_tensor_tensor(out=m[:, 3], in0=m[:, 2], scalar=1.0 / D, in1=m[:, 0],
                                               op0=ALU.mult, op1=ALU.add).then_inc(s["mom"], 1)
                nc.vector.tensor_scalar(m[:, 4], m[:, 1], 0.5, None, ALU.mult).then_inc(s["mom"], 1)
                if more:
                    one_hot(q + 2, par, 2)
                dve.wait_ge(s["mom"], 6 * q + 6)
                inverse_root(dve, m[:, 3], [nwt[:, par, i] for i in range(5)], s["newt"], q * NEWTON_OPS,
                             [lambda u=u: one_hot(q + 2, par, u) for u in (3, 4)] if more else [])
                dve.wait_ge(s["newt"], (q + 1) * NEWTON_OPS)
                for u in range(QT):
                    last = nc.vector.tensor_scalar(act[:, par, u, :], act[:, par, u, :], m[:, 4, u:u + 1],
                                                   nwt[:, par, 4, u:u + 1], ALU.subtract, ALU.mult)
                last.then_inc(s["norm"], 1)

            def compare(q, par):
                dve.wait_ge(s["keyt"], q + 1)
                if later(q, 2):
                    dve.wait_ge(s["ded"], q - 1)
                nc.vector.tensor_tensor(same[:, par, :, :], ps[:, PK, :].rearrange("p (u n) -> p u n", u=QT),
                                        key[:, par, :].unsqueeze(2).to_broadcast([P, QT, P]), ALU.is_equal)\
                    .then_inc(s["same"], 1)

            def count_before(q, par):
                dve.wait_ge(s["same"], q + 1)
                if later(q, 1):
                    dve.wait_ge(s["dup"], QT * q)
                for u in range(QT):
                    nc.vector.tensor_tensor_reduce(out=scr[:, u, :], in0=same[:, par, u, :], in1=lower[:, :],
                                                   scale=1.0, scalar=0.0, op0=ALU.mult, op1=ALU.add,
                                                   accum_out=dup[:, par, u:u + 1]).then_inc(s["dup"], 1)
                nc.vector.tensor_tensor(dif[:, par, :, 0], trash[:, :], key[:, par, :], ALU.subtract)\
                    .then_inc(s["dif"], 1)

            def sum_rows(q, par):
                dve.wait_ge(s["dup"], QT * (q + 1))
                dve.wait_ge(s["dif"], 2 * q + 1)
                nc.vector.scalar_tensor_tensor(out=dif[:, par, :, 1], in0=dup[:, par, :], scalar=0.5,
                                               in1=dif[:, par, :, 0], op0=ALU.is_gt, op1=ALU.mult)\
                    .then_inc(s["dif"], 1)
                if later(q, 2):
                    dve.wait_ge(s["added"], (q - 1) * (16 * QT))
                dve.wait_ge(s["dif"], 2 * q + 2)
                nc.vector.tensor_tensor(sidx[:, par, :], dif[:, par, :, 1], key[:, par, :], ALU.add)\
                    .then_inc(s["sidx"], 1)

            def step_0(q, par):
                o = 1 - par
                if live(q, QUADS):
                    pre(q, par)
                if live(q - 1, QUADS):
                    compare(q - 1, o)
                if live(q, QUADS):
                    stage_keys(q, par)
                if live(q - 1, QUADS):
                    count_before(q - 1, o)
                if live(q + 2, QUADS):
                    stage(q + 2, par, 0)
                if live(q - 1, QUADS):
                    sum_rows(q - 1, o)
                if live(q, QUADS):
                    norm(q, par)
                elif live(q + 2, QUADS):
                    for u in range(QT + 1):
                        one_hot(q + 2, par, u)
            dve.wait_ge(s_visit, 10 + 2 * PARTS - 1)
            steps(dve, QUADS, 1, step_0, ahead=2)

            def hidden(q, par):
                dve.wait_ge(t["hmm"], q + 1)
                if later(q, 2):
                    dve.wait_ge(t["hid"], q - 1)
                nc.vector.tensor_tensor(hpre[0:NB, par, :], ps[0:NB, PM + par, 0:D], ub1b[0:NB, :], ALU.add)\
                    .then_inc(t["hpre"], 1)

            def result(q, par, l):
                row = rows[0:NB, bass.ds(q, 1), 0:D].rearrange("p a d -> p (a d)")
                dve.wait_ge(t["omm"], q + 1)
                nc.vector.tensor_tensor(hpre2[0:NB, par, :], ps[0:NB, PK, par * D:(par + 1) * D],
                                        (ub2b if l == 0 else blb)[0:NB, :], ALU.add).then_inc(t["oadd"], 1)
                dve.wait_ge(t["oadd"], q + 1)
                if l == 0:
                    dve.wait_ge(t["xcopy"], q + 1)
                    nc.vector.scalar_tensor_tensor(out=row, in0=row, scalar=2.0, in1=hpre2[0:NB, par, :],
                                                   op0=ALU.mult, op1=ALU.add).then_inc(t["res"], 1)
                else:
                    dve.wait_ge(t[f"load{par}"], half_count(q) * 32)
                    nc.vector.scalar_tensor_tensor(out=row, in0=hpre2[0:NB, par, :], scalar=0.0, in1=xin[0:NB, par, :],
                                                   op0=ALU.max, op1=ALU.add).then_inc(t["res"], 1)
                dve.wait_ge(t["res"], q + 1)
                dve.sem_inc(s_turn_dve, 1)
                nc.vector.bn_stats(bst2[:, par, :], row).then_inc(t["bst"], 1)
                dve.wait_ge(t["bst"], q + 1)
                dve.sem_inc(s_turn_dve, 1)
                nc.vector.bn_aggr(mv2[:, par, :], bst2[:, par, :]).then_inc(t["aggr"], 1)
                dve.wait_ge(t["aggr"], q + 1)
                dve.sem_inc(s_turn_dve, 1)
                nc.vector.tensor_copy(mst[:, bass.ds(q, 1), :].rearrange("p a d -> p (a d)"), mv2[:, par, :])\
                    .then_inc(t["stat"], 1)

            def normalise_all():
                dve.wait_ge(t["stat"], BLOCKS)
                inverse_root(dve, mst[:, :, 1], [nwb[:, i] for i in range(5)], t["newt"], 0)
                dve.wait_ge(t["newt"], NEWTON_OPS)

                def normalise(q, par):
                    row = rows[0:NB, bass.ds(q, 1), 0:D].rearrange("p a d -> p (a d)")
                    nc.vector.tensor_scalar(row, row, mst[:, bass.ds(q, 1), 0], nwb[:, 4, bass.ds(q, 1)],
                                            ALU.subtract, ALU.mult).then_inc(t["norm"], 1)
                steps(dve, BLOCKS, 0, normalise)

            t = k[0]

            def add_tables(q, par):
                dve.wait_ge(t[f"load{par}"], half_count(q) * (32 * (TABLES + 1)))
                nc.vector.tensor_tensor(half[0:NB, par, :, :], blk[0:NB, par, 0:2, :], blk[0:NB, par, 2:4, :], ALU.add)\
                    .then_inc(t["half"], 1)
                dve.wait_ge(t["half"], q + 1)
                if later(q, 2):
                    dve.wait_ge(t["cols"], q - 1)
                nc.vector.tensor_tensor(agg[0:NB, par, :], half[0:NB, par, 0, :], half[0:NB, par, 1, :], ALU.add)\
                    .then_inc(t["agg"], 1)

            def block_0(q, par):
                if live(q, BLOCKS):
                    add_tables(q, par)
                if live(q - 1, BLOCKS):
                    hidden(q - 1, 1 - par)
                if live(q - 3, BLOCKS):
                    result(q - 3, 1 - par, 0)
            steps(dve, BLOCKS, 3, block_0)
            normalise_all()

            s = e[1]
            dve.wait_ge(s_x1st, 32 * BLOCKS)
            nc.vector.memset(rows[0:NB, :, 0:CW], 0.0).then_inc(s_ones, 1)
            nc.vector.memset(msg[:, :, :, D:CW], 1.0).then_inc(s_ones, 1)

            def one_hot_1(q, par):
                if later(q, 2):
                    dve.wait_ge(s["agg"], QT * (q - 1))
                    dve.sem_inc(s_turn_dve, 1)
                for u in range(QT):
                    last = nc.vector.tensor_scalar(same[:, par, u, 0:NB], nodes[:, :], vloc[:, bass.ds(q * QT + u, 1)],
                                                   None, ALU.is_equal)
                last.then_inc(s["hot"], 1)

            def accumulate(q, par):
                to = [dve.value_load(vblk[0:1, bass.ds(q * QT + u, 1)], min_val=0, max_val=BLOCKS - 1)
                      for u in range(QT)]
                for u in range(QT):
                    row = rows[0:NB, bass.ds(to[u], 1), 0:CW].rearrange("p a d -> p (a d)")
                    dve.wait_ge(s["agg"], q * QT + u + 1)
                    if u > 0 or later(q, 1):
                        dve.wait_ge(s["acc"], q * QT + u)
                    nc.vector.tensor_tensor(row, ps[0:NB, u, 0:CW], row, ALU.add).then_inc(s["acc"], 1)

            def step_1(q, par):
                if live(q + 1, QUADS):
                    stage(q + 1, 1 - par, 1)
                    one_hot_1(q + 1, 1 - par)
                if live(q, QUADS):
                    accumulate(q, par)
            dve.wait_ge(s_ones, 2)
            steps(dve, QUADS, 0, step_1, ahead=1)

            t = k[1]

            def mean(q, par):
                sums_ = rows[0:NB, bass.ds(q, 1), 0:CW].rearrange("p a d -> p (a d)")
                nc.vector.tensor_scalar(cnt[0:NB, par, 0:1], sums_[:, D:CW], 1.0, None, ALU.max).then_inc(t["cnt"], 1)
                dve.wait_ge(t["cnt"], 2 * q + 1)
                nc.vector.reciprocal(cnt[0:NB, par, 1:2], cnt[0:NB, par, 0:1]).then_inc(t["cnt"], 1)
                dve.wait_ge(t["cnt"], 2 * q + 2)
                if later(q, 2):
                    dve.wait_ge(t["cols"], q - 1)
                nc.vector.tensor_scalar(agg[0:NB, par, :], sums_[:, 0:D], cnt[0:NB, par, 1:2], None, ALU.mult)\
                    .then_inc(t["agg"], 1)

            def block_1(q, par):
                if live(q, BLOCKS):
                    mean(q, par)
                if live(q - 1, BLOCKS):
                    result(q - 1, 1 - par, 1)
            dve.wait_ge(s["acc"], QUADS * QT)
            steps(dve, BLOCKS, 1, block_1)
            normalise_all()


_INS = ["x", "src", "dst", "edge_weight1", "L0_gnn_mW1", "L0_gnn_mb1", "L0_gnn_ln_g", "L0_gnn_ln_b", "L0_gnn_mW2",
        "L0_gnn_mb2", "L0_gnn_uW1", "L0_gnn_ub1", "L0_gnn_uW2", "L0_gnn_ub2", "L1_gnn_W", "L1_gnn_b"]


def kernel(**inputs):
    import numpy as _np
    import concourse.bacc as _bacc
    from concourse import mybir as _mybir
    from concourse.bass_utils import run_bass_kernel_spmd as _run

    nc = _bacc.Bacc("TRN2", target_bir_lowering=False, num_devices=1)
    arrays, args = {}, []
    for name in _INS:
        a = _np.ascontiguousarray(inputs[name])
        arrays[f"in_{name}_dram"] = a
        args.append(nc.dram_tensor(f"in_{name}_dram", a.shape, _mybir.dt.from_np(a.dtype), kind="ExternalInput").ap())
    args.append(nc.dram_tensor("out_0_dram", (N, D), _mybir.dt.float32, kind="ExternalOutput").ap())
    gnn(nc, *args)
    r = _run(nc, [arrays], core_ids=[0])
    return r.results[0]["out_0_dram"]
```

```python
import concourse.bass as bass
from concourse import mybir
from contextlib import ExitStack

N = 6250
D = 256
E = 106250
P = 128
H = D // P
LN_EPS = 1e-5

QT = 4
TILES = -(-E // P)
CHUNKS = -(-TILES // P)
FULL = E // P
REST = E - FULL * P
NB = 125
BLOCKS = N // NB
QUADS = -(-(TILES + BLOCKS - 1) // QT)
VISITS = QUADS * QT
ROWS = N + NB
PAD = N
SUMROWS = 50 * P
TABLES = QT
PARTS = 3
CW = D + 1
ROUND = 1.5 * 2.0 ** 23
MAGIC = 0x5F3759DF
XSLOTS = 4
NEWTON = 3
NEWTON_OPS = 3 + 3 * NEWTON
assert BLOCKS * NB == N and SUMROWS >= N + P and REST > 0 and NB + PARTS == P and D == 256


def gnn(nc, x, src, dst, edge_w, mW1, mb1, ln_g, ln_b, mW2, mb2, uW1, ub1, uW2, ub2, W, b, out):
    f32, i32, bf16 = mybir.dt.float32, mybir.dt.int32, mybir.dt.bfloat16
    ALU = mybir.AluOpType
    ACT = mybir.ActivationFunctionType
    AX = mybir.AxisListType

    p_tab = nc.dram_tensor("p_tab", (ROWS, D), f32, kind="Internal").ap()
    rec_tab = nc.dram_tensor("rec_tab", (CHUNKS * P * P, 3), f32, kind="Internal").ap()
    x1_tab = nc.dram_tensor("x1_tab", (ROWS, D), f32, kind="Internal").ap()
    sums = [nc.dram_tensor(f"sum_{r}", (SUMROWS, D), f32, kind="Internal").ap() for r in range(TABLES)]

    with ExitStack() as ctx:
        def sb(name, shape, dt=f32):
            return ctx.enter_context(nc.sbuf_tensor(name, shape, dt))

        def sem(name):
            return ctx.enter_context(nc.semaphore(name))

        ident = sb("ident", [P, P])
        identh = sb("identh", [P, P], bf16)
        lower = sb("lower", [P, P])
        nextp = sb("nextp", [P, P])
        wrap = sb("wrap", [P, P])
        zeros = sb("zeros", [P, D])
        ones = sb("ones", [P, P], bf16)
        onesf = sb("onesf", [P, P])
        nodes = sb("nodes", [P, NB], bf16)
        w1 = sb("w1", [P, 2 * H, D])
        w2 = sb("w2", [P, H, D])
        u1 = sb("u1", [P, 2 * H, D])
        u2 = sb("u2", [P, H, D])
        wl = sb("wl", [P, H, D])
        wt = sb("wt", [P, H, D])
        b1b = sb("b1b", [P, D])
        b2r = sb("b2r", [P, D], bf16)
        ub1b = sb("ub1b", [P, D])
        ub2b = sb("ub2b", [P, D])
        blb = sb("blb", [P, D])
        gb = sb("gb", [P, H, 2])
        big = sb("big", [P, BLOCKS, PARTS, D], bf16)
        rows = big[:, :, :, :].rearrange("p j k d -> p (j k d)").bitcast(f32)\
            .rearrange("p (j c) -> p j c", j=BLOCKS)
        vsrc = sb("vsrc", [P, VISITS], i32)
        vkey = sb("vkey", [P, VISITS])
        vkeyh = sb("vkeyh", [P, 2, VISITS], bf16)
        vloc = sb("vloc", [P, VISITS])
        vwgt = sb("vwgt", [P, VISITS, PARTS], bf16)
        vblk = sb("vblk", [P, VISITS], i32)
        trash_i = sb("trash_i", [P, QT], i32)
        trash = sb("trash", [P, QT])
        bstb = sb("bstb", [NB, BLOCKS, 6])
        momb = sb("momb", [NB, 3, BLOCKS])
        nwb = sb("nwb", [NB, 4, BLOCKS])
        cnt = sb("cnt", [NB, 2, BLOCKS])

        work = sb("work", [P, 12544])
        at_ = [0]

        def cut(shape, dt=f32, parts=P):
            n = 1
            for m in shape:
                n *= m
            words = n if dt != bf16 else n // 2
            ap = work[:, at_[0]:at_[0] + words]
            at_[0] += words
            assert at_[0] <= 12544, at_[0]
            ap = ap if dt == f32 else ap.bitcast(dt)
            names = "abcd"[:len(shape)]
            ap = ap.rearrange(f"p ({' '.join(names)}) -> p {' '.join(names)}", **dict(zip(names, shape)))
            return ap[0:parts]

        gat = cut([2, QT, D])
        act = cut([2, QT, D])
        zt = cut([2, H, QT * P])
        msg = cut([2, QT, CW + 3])
        tot = cut([2, QT, D])
        same = cut([2, QT, P])
        hot = cut([2, QT, P], bf16)
        hott = cut([2, QT, P], bf16)
        assert at_[0] <= 12544
        at_[0] = 0
        loaded = cut([3, CHUNKS, P])
        ends = cut([2, CHUNKS, P])
        pick = cut([2, 2, VISITS])
        vdst = cut([VISITS])
        wrest = cut([2, VISITS])
        viota = cut([VISITS])
        at_[0] = 0
        blk = cut([2, TABLES, D])
        half = cut([2, 2, D])
        agg = cut([2, D])
        col = cut([2, 2 * H, P])
        xin = cut([2, D])
        hpre = cut([2, D])
        hpre2 = cut([2, D])
        hid = cut([2, D])
        hcol = cut([2, H, P])
        pcol = sb("pcol", [P, 2, H, P])
        pxin = sb("pxin", [NB, XSLOTS, D])
        prow = sb("prow", [NB, 2, D])
        qres = sb("qres", [NB, 2, D])
        w1cf = sb("w1cf", [P, 2, D])
        w1cp = sb("w1cp", [P, PARTS, D], bf16)
        b2f = sb("b2f", [P, 3, D])
        b2p = sb("b2p", [P, PARTS, D], bf16)

        scr = sb("scr", [P, QT, P])
        idx = sb("idx", [P, 2, QT], i32)
        key = sb("key", [P, 2, QT])
        loc = sb("loc", [P, 2, QT])
        keyh = sb("keyh", [P, 2, 2, QT], bf16)
        dup = sb("dup", [P, 2, QT])
        dif = sb("dif", [P, 2, QT, 2])
        sidx = sb("sidx", [P, 2, QT], i32)
        bst = sb("bst", [P, 2, QT, 6])
        mom = sb("mom", [P, 2, 5, QT])
        nwt = sb("nwt", [P, 2, 4, QT])
        tnum_i = sb("tnum_i", [P, CHUNKS], i32)
        viota_i = sb("viota_i", [P, VISITS], i32)
        tnum = sb("tnum", [P, CHUNKS])
        thi = sb("thi", [P, 4, CHUNKS])
        tprev = sb("tprev", [P, CHUNKS])
        first_v = sb("first_v", [P, CHUNKS])
        next_v = sb("next_v", [P, CHUNKS])
        down = sb("down", [P, CHUNKS + 1])
        down_i = sb("down_i", [P, 1], i32)

        scratch = big[:, :, :, :].rearrange("p j k d -> p (j k d)").bitcast(f32)
        W_ALL = CHUNKS * P
        f_blk, f_mask, f_pos, f_cum0, f_cum1 = (scratch[:, i * W_ALL:(i + 1) * W_ALL] for i in range(5))
        f_cum = (f_cum0, f_cum1)
        f_pos_i = scratch[:, 5 * W_ALL:6 * W_ALL].bitcast(i32)
        f_rec = scratch[:, 6 * W_ALL:9 * W_ALL].rearrange("p (c a) -> p c a", a=3)
        f_sorted = scratch[:, 9 * W_ALL:12 * W_ALL]
        f_run = sb("f_run", [P, 2])
        f_slot_i = sb("f_slot_i", [P, 1], i32)
        f_slot = sb("f_slot", [P, 3])

        ps = ctx.enter_context(nc.psum_tensor("ps", [P, 7, 512], f32))
        psh = ctx.enter_context(nc.psum_tensor("psh", [P, QT, P], bf16))
        PM, PZ, PP, PK = 0, 2, 4, 6

        def flat(ap):
            return ap.rearrange("p a b -> p (a b)")

        SPLIT = ((0, 112), (112, NB))
        GROUP = 10
        STORES = 32 * (BLOCKS // GROUP)

        def by_place(rows_, group):
            return rows_[group * GROUP * NB:(group + 1) * GROUP * NB, :].rearrange("(j p) d -> p j d", p=NB)

        s_const, s_constc, s_zeroed, s_pad = sem("s_const"), sem("s_constc"), sem("s_zeroed"), sem("s_pad")
        s_edges, s_weights, s_tables = sem("s_edges"), sem("s_weights"), sem("s_tables")
        s_ends, s_tile, s_prev, s_range = sem("s_ends"), sem("s_tile"), sem("s_prev"), sem("s_range")
        s_done_g, s_count, s_blk, s_pick, s_picked, s_visit = (sem("s_done_g"), sem("s_count"), sem("s_blk"),
                                                               sem("s_pick"), sem("s_picked"), sem("s_visit"))
        s_bias, s_wpart, s_wrow, s_wtr, s_wt = sem("s_bias"), sem("s_wpart"), sem("s_wrow"), sem("s_wtr"), sem("s_wt")
        s_xload = [sem(f"s_xload{i}") for i in range(XSLOTS)]
        s_xt, s_xtev, s_pqmm, s_prow, s_q1, s_qr, s_q2, s_q3 = (
            sem("s_xt"), sem("s_xtev"), sem("s_pqmm"), sem("s_prow"), sem("s_q1"), sem("s_qr"), sem("s_q2"), sem("s_q3"))
        s_pst = [sem("s_pst0"), sem("s_pst1")]
        s_turn_pool, s_turn_dve, s_turn_act = sem("s_turn_pool"), sem("s_turn_dve"), sem("s_turn_act")
        s_down, s_flag, f_ends, f_tile, f_prev, f_range = (sem("s_down"), sem("s_flag"), sem("f_ends"), sem("f_tile"),
                                                           sem("f_prev"), sem("f_range"))
        f_seq, f_count, f_based, f_ready, f_copied, f_done, f_load, f_back = (
            sem("f_seq"), sem("f_count"), sem("f_based"), sem("f_ready"), sem("f_copied"), sem("f_done"), sem("f_load"),
            sem("f_back"))
        s_xrows, s_x1st, s_out, s_ones = sem("s_xrows"), sem("s_x1st"), sem("s_out"), sem("s_ones")

        EDGE = [["staged", "gat0", "gat1", "hot", "hott", "hev", "keyt", "apart", "same", "dup", "dif", "sidx", "qexp", "pre",
                 "keys", "placed", "silu", "bst", "mom", "newt", "norm", "ztr", "zev", "mm", "msg", "ded", "tot", "added"],
                ["staged", "gat0", "gat1", "hot", "agg", "acc"]]
        e = [{n: sem(f"e{l}_{n}") for n in EDGE[l]} for l in range(2)]
        BLOCK = ["load0", "load1", "xcopy", "half", "agg", "cnt", "cols", "colev", "hmm", "hpre", "hid", "hcols", "hcolev",
                 "omm", "oadd", "res", "stat", "mom", "newt", "norm"]
        k = [{n: sem(f"b{l}_{n}") for n in BLOCK} for l in range(2)]

        block = ctx.enter_context(nc.Block())

        def steps(eng, n, lag, step, ahead=0, by=2, slots=2):
            lo = max(4, (lag + 3) // by * by)
            hi = (n - ahead) // by * by
            for q in range(-ahead, lo):
                step(q, q % slots)
            with eng.Fori(lo // by, hi // by) as it:
                for k_ in range(by):
                    step(it * by + k_, k_ % slots)
            for q in range(hi, n + lag):
                step(q, q % slots)

        def live(q, n):
            return not isinstance(q, int) or 0 <= q < n

        def half_count(q):
            return q // 2 + 1

        def later(q, n):
            return not isinstance(q, int) or q >= n

        def inverse_root(dve, v, w, sem_, at, beside=lambda i: None):
            nc.vector.tensor_scalar(w[2].bitcast(i32), v.bitcast(i32), 1, None, ALU.logical_shift_right)\
                .then_inc(sem_, 1)
            nc.vector.tensor_scalar(w[1], v, -0.5, None, ALU.mult).then_inc(sem_, 1)
            beside(0)
            dve.wait_ge(sem_, at + 1)
            nc.vector.tensor_scalar(w[3].bitcast(i32), w[2].bitcast(i32), -1.0, float(MAGIC), ALU.mult, ALU.add)\
                .then_inc(sem_, 1)
            beside(1)
            for i in range(NEWTON):
                dve.wait_ge(sem_, at + 3 + 3 * i)
                nc.vector.tensor_tensor(w[2], w[3], w[3], ALU.mult).then_inc(sem_, 1)
                beside(2 + 3 * i)
                dve.wait_ge(sem_, at + 4 + 3 * i)
                nc.vector.tensor_tensor(w[0], w[2], w[1], ALU.mult).then_inc(sem_, 1)
                beside(3 + 3 * i)
                dve.wait_ge(sem_, at + 5 + 3 * i)
                nc.vector.scalar_tensor_tensor(out=w[3], in0=w[0], scalar=1.5, in1=w[3], op0=ALU.add, op1=ALU.mult)\
                    .then_inc(sem_, 1)
                beside(4 + 3 * i)

        def visit_blocks(eng, q, regs):
            eng.load(regs, vblk[0:1, bass.ds(q * QT, QT)])
            return [eng.snap(reg, min_val=0, max_val=BLOCKS - 1) for reg in regs]

        def tiles_down(eng):
            eng.wait_ge(s_flag, 1)
            return eng.value_load(down_i[0:1, 0:1], min_val=0, max_val=TILES)

        @block.sync
        def _(sp):
            sp.wait_ge(s_pad, 3)
            last, left = CHUNKS - 1, FULL - (CHUNKS - 1) * P
            for a, arr in enumerate((src, dst, edge_w.rearrange("e o -> (e o)"))):
                dest = loaded[:, a] if a == 2 else loaded[:, a].bitcast(i32)
                sp.dma_start(dest[:, 0:last, :], arr[0:last * P * P].rearrange("(k r e) -> r k e", r=P, e=P))\
                    .then_inc(s_edges, 16)
                sp.dma_start(dest[0:left, last, :], arr[last * P * P:FULL * P].rearrange("(r e) -> r e", e=P))\
                    .then_inc(s_edges, 16)
                sp.dma_start(dest[left:left + 1, last, 0:REST], arr[FULL * P:E].rearrange("(r e) -> r e", e=REST))\
                    .then_inc(s_edges, 16)
            for dest, arr in ((w1, mW1[0:2 * D, :]), (w2, mW2), (u1, uW1), (u2, uW2), (wl, W)):
                sp.dma_start(dest[:, :, :], arr.rearrange("(k p) d -> p k d", p=P)).then_inc(s_weights, 16)
            for dest, row in ((w1cf[:, 0, :], mW1[2 * D:2 * D + 1, :]), (b1b[:, :], mb1), (b2f[:, 0, :], mb2),
                              (ub1b[:, :], ub1), (ub2b[:, :], ub2), (blb[:, :], b)):
                row = row if len(row.shape) == 2 else row.rearrange("(a n) -> a n", a=1)
                sp.dma_start(dest, row.to_broadcast([P, D])).then_inc(s_weights, 16)
            for a, row in enumerate((ln_g, ln_b)):
                for h in range(H):
                    sp.dma_start(gb[:, h, a:a + 1], row[h * P:(h + 1) * P].rearrange("(p a) -> p a", a=1))\
                        .then_inc(s_weights, 16)
            sp.wait_ge(s_zeroed, 1)
            for t in sums:
                sp.dma_start(t.rearrange("(p a) d -> p a d", p=P),
                             zeros[:, :].unsqueeze(1).to_broadcast([P, SUMROWS // P, D])).then_inc(s_tables, 16)
            for t in (p_tab, x1_tab):
                sp.dma_start(t[N:ROWS, :], zeros[0:NB, :]).then_inc(s_tables, 16)
            with sp.If(tiles_down(sp) > 0):
                sp.wait_ge(f_done, 16 * W_ALL)
                sp.dma_start(f_sorted.rearrange("p (k e) -> p k e", k=CHUNKS),
                             rec_tab.rearrange("(k r e) a -> r k (e a)", r=P, e=P)).then_inc(f_load, 16)
            def pq_step(q, k):
                n = q + XSLOTS - 1
                if live(n, BLOCKS):
                    if later(n, XSLOTS):
                        sp.wait_ge(s_xt, q)
                    for a, z in SPLIT:
                        sp.dma_start(pxin[a:z, (k - 1) % XSLOTS, :], x[bass.ds(n * NB + a, z - a), :])\
                            .then_inc(s_xload[(k - 1) % XSLOTS], 16)
                if live(q - 1, BLOCKS):
                    o = (k - 1) % 2
                    sp.wait_ge(s_prow, q)
                    for a, z in SPLIT:
                        sp.dma_start(p_tab[bass.ds((q - 1) * NB + a, z - a), :], prow[a:z, o, :])\
                            .then_inc(s_pst[o], 16)
            steps(sp, BLOCKS, 1, pq_step, ahead=XSLOTS - 1, by=XSLOTS, slots=XSLOTS)

            sp.wait_ge(s_wpart, 5)
            sp.dma_start(big[NB:P, :, :, :].rearrange("p j k d -> p j (k d)"),
                         w1cp[0:PARTS, :, :].rearrange("p k d -> p (k d)").unsqueeze(1)
                         .to_broadcast([PARTS, BLOCKS, PARTS * D])).then_inc(s_wrow, 16)

            sp.wait_ge(e[0]["qexp"], QUADS)
            for g in range(BLOCKS // GROUP):
                for a, z in SPLIT:
                    sp.dma_start(rows[a:z, g * GROUP:(g + 1) * GROUP, 0:D], by_place(x, g)[a:z]).then_inc(s_xrows, 16)
            sp.wait_ge(e[0]["added"], 16 * QT * QUADS)

            def load_0(q, par):
                if later(q, 2):
                    sp.wait_ge(k[0]["half"], q - 1)
                for r in range(TABLES):
                    sp.dma_start(blk[:, par, r, :], sums[r][bass.ds(q * NB, P), :]).then_inc(k[0][f"load{par}"], 16)
            steps(sp, BLOCKS, 0, load_0)

            def store(l, to):
                for g in range(BLOCKS // GROUP):
                    sp.wait_ge(k[l]["norm"], GROUP * (g + 1))
                    for a, z in SPLIT:
                        sp.dma_start(by_place(to, g)[a:z], rows[a:z, g * GROUP:(g + 1) * GROUP, 0:D])\
                            .then_inc(s_x1st if l == 0 else s_out, 16)
            store(0, x1_tab[0:N, :])

            sp.wait_ge(s_x1st, STORES)

            def load_1(q, par):
                if later(q, 2):
                    sp.wait_ge(k[1]["res"], q - 1)
                sp.dma_start(xin[:, par, :], x1_tab[bass.ds(q * NB, P), :]).then_inc(k[1][f"load{par}"], 16)
            sp.wait_ge(e[1]["acc"], QUADS * QT)
            steps(sp, BLOCKS, 0, load_1)
            store(1, out)
            sp.wait_ge(s_out, STORES)

        @block.gpsimd
        def _(pool):
            nc.gpsimd.memset(loaded[:, 0:2, CHUNKS - 1, :].bitcast(i32), PAD).then_inc(s_pad, 2)
            nc.gpsimd.memset(loaded[:, 2, CHUNKS - 1, :], 0.0).then_inc(s_pad, 1)
            nc.gpsimd.memset(zeros[:, :], 0.0).then_inc(s_zeroed, 1)
            nc.gpsimd.memset(ident[:, :], 0.0).then_inc(s_constc, 1)
            nc.gpsimd.memset(lower[:, :], 1.0).then_inc(s_constc, 1)
            nc.gpsimd.memset(nextp[:, :], 0.0).then_inc(s_constc, 1)
            nc.gpsimd.memset(wrap[:, :], 0.0).then_inc(s_constc, 1)
            nc.gpsimd.memset(ones[:, :], 1.0).then_inc(s_const, 1)
            nc.gpsimd.memset(onesf[:, :], 1.0).then_inc(s_const, 1)
            nc.gpsimd.iota(trash_i[:, :], pattern=[[0, QT]], base=N, channel_multiplier=1).then_inc(s_constc, 1)
            nc.gpsimd.iota(tnum_i[:, :], pattern=[[P, CHUNKS]], base=0, channel_multiplier=1).then_inc(s_constc, 1)
            nc.gpsimd.iota(viota_i[:, :], pattern=[[1, VISITS]], base=0, channel_multiplier=0).then_inc(s_constc, 1)
            pool.wait_ge(s_constc, 7)
            for mat, op, fill, base in ((ident, ALU.not_equal, 1.0, 0), (lower, ALU.is_gt, 0.0, 0),
                                        (nextp, ALU.not_equal, 1.0, 1)):
                nc.gpsimd.affine_select(out=mat[:, :], in_=mat[:, :], compare_op=op, fill=fill, base=base,
                                        pattern=[[-1, P]], channel_multiplier=1).then_inc(s_const, 1)
            nc.gpsimd.affine_select(out=wrap[:, :], in_=wrap[:, :], compare_op=ALU.not_equal, fill=1.0, base=1 - P,
                                    pattern=[[P, P]], channel_multiplier=1).then_inc(s_const, 1)
            nc.gpsimd.tensor_copy(trash[:, :], trash_i[:, :]).then_inc(s_const, 1)
            nc.gpsimd.tensor_copy(tnum[:, :], tnum_i[:, :]).then_inc(s_const, 1)
            pool.wait_ge(s_const, 8)
            nc.gpsimd.tensor_copy(identh[:, :], ident[:, :]).then_inc(s_const, 1)
            nc.gpsimd.tensor_copy(nodes[:, :], viota_i[:, 0:NB]).then_inc(s_const, 1)
            with pool.If(tiles_down(pool) > 0):
                pool.wait_ge(f_ready, 5)

                def place(c):
                    nc.gpsimd.tensor_copy(f_slot_i[:, :], f_pos_i[:, bass.ds(c, 1)]).then_inc(f_copied, 1)
                    nc.gpsimd.tensor_copy(f_slot[:, :], f_rec[:, bass.ds(c, 1), :].rearrange("p a d -> p (a d)"))\
                        .then_inc(f_copied, 1)
                    pool.wait_ge(f_copied, 2 * (c + 1))
                    pool.sem_inc(s_turn_pool, 1)
                    pool.indirect_dma_start(
                        out=rec_tab[:, :], out_offset=bass.IndirectOffsetOnAxis(ap=f_slot_i[:, 0:1], axis=0),
                        in_=f_slot[:, :], in_offset=None).then_inc(f_done, 16)
                place(0)
                with pool.Fori(1, W_ALL) as c:
                    pool.wait_ge(f_done, 16 * c)
                    pool.sem_inc(s_turn_pool, 1)
                    place(c)
            pool.wait_ge(s_tables, 16 * (TABLES + 2))
            for par in (0, 1):
                pool.wait_ge(s_pst[par], 32 * BLOCKS // 2)

            def gather(l, table, slots):
                def step(q, par):
                    pool.wait_ge(e[l]["staged"], q + 1)
                    if l == 0 and later(q, 2):
                        pool.wait_ge(e[l]["pre"], 2 * (q - 1))
                    for u in range(QT):
                        if l == 1 and later(q, 2):
                            pool.wait_ge(e[l]["agg"], (q - 2) * QT + u + 1)
                        if u == 0 or (l == 1 and later(q, 2)):
                            pool.sem_inc(s_turn_pool, 1)
                        pool.indirect_dma_start(
                            out=slots[:, par, u, 0:D], out_offset=None, in_=table[:, :],
                            in_offset=bass.IndirectOffsetOnAxis(ap=idx[:, par, u:u + 1], axis=0))\
                            .then_inc(e[l][f"gat{par}"], 16)
                return step

            def add(q, par):
                pool.wait_ge(e[0]["tot"], q + 1)
                pool.wait_ge(e[0]["sidx"], q + 1)
                if later(q, 1):
                    pool.wait_ge(e[0]["added"], q * (16 * QT))
                pool.sem_inc(s_turn_pool, 1)
                for u in range(QT):
                    pool.indirect_dma_start(
                        out=sums[u][:, :], in_=tot[:, par, u, :], in_offset=None,
                        out_offset=bass.IndirectOffsetOnAxis(ap=sidx[:, par, u:u + 1], axis=0),
                        compute_op=ALU.add).then_inc(e[0]["added"], 16)

            gather_0 = gather(0, p_tab, gat)

            def step_0(q, par):
                if live(q + 1, QUADS):
                    gather_0(q + 1, 1 - par)
                if live(q - 2, QUADS):
                    add(q - 2, par)
            steps(pool, QUADS, 2, step_0, ahead=1, by=4)

            pool.wait_ge(s_xrows, STORES)

            def copy_x(q, par):
                if later(q, 2):
                    pool.wait_ge(k[0]["cols"], q - 1)
                    pool.sem_inc(s_turn_pool, 1)
                nc.gpsimd.tensor_copy(xin[0:NB, par, :], rows[0:NB, bass.ds(q, 1), 0:D]
                                      .rearrange("p a d -> p (a d)")).then_inc(k[0]["xcopy"], 1)
            steps(pool, BLOCKS, 0, copy_x)
            pool.wait_ge(s_x1st, STORES)
            pool.wait_ge(s_tables, 16 * (TABLES + 2))
            steps(pool, QUADS, 0, gather(1, x1_tab, msg), by=4)

        @block.tensor
        def _(pe):
            pe.wait_ge(s_const, 10)
            pe.wait_ge(s_weights, 16 * 15)
            for kd in range(H):
                for kh in range(H):
                    last = nc.tensor.transpose(ps[:, PK, (kd * H + kh) * P:(kd * H + kh + 1) * P],
                                               wl[:, kh, kd * P:(kd + 1) * P], ident[:, :])
            last.then_inc(s_wtr, 1)
            pe.wait_ge(s_wt, 1)
            def tile_before(tile, prev):
                pe.wait_ge(tile, 4)
                nc.tensor.matmul(ps[:, PK, 0:CHUNKS], nextp[:, :], thi[:, 3, :], start=True, stop=False)
                nc.tensor.matmul(ps[:, PK, 1:CHUNKS], wrap[:, :], thi[:, 3, 0:CHUNKS - 1], start=False, stop=True)\
                    .then_inc(prev, 1)
            tile_before(s_tile, s_prev)
            pe.wait_ge(s_down, 2)
            nc.tensor.matmul(ps[:, PP, 0:1], onesf[:, :], down[:, CHUNKS:CHUNKS + 1], start=True, stop=True)\
                .then_inc(s_down, 1)
            with pe.If(tiles_down(pe) > 0):
                def counts(q):
                    pe.wait_ge(f_count, q + 1)
                    nc.tensor.matmul(ps[:, PZ, 0:1], lower[:, :], f_cum[0][:, W_ALL - 1:W_ALL], start=True, stop=True)
                    nc.tensor.matmul(ps[:, PZ, 1:2], onesf[:, :], f_cum[0][:, W_ALL - 1:W_ALL], start=True, stop=True)\
                        .then_inc(f_based, 1)
                with pe.Fori(0, BLOCKS + 1) as q:
                    counts(q)
                tile_before(f_tile, f_prev)
            HV = VISITS // 2
            for c in range(CHUNKS):
                pe.wait_ge(s_done_g, c + 1)
                for v in range(2):
                    last = nc.tensor.matmul(ps[:, v, 0:HV], onesf[:, :], pick[:, c % 2, 0, v * HV:(v + 1) * HV],
                                            start=c == 0, stop=c == CHUNKS - 1)
                last.then_inc(s_count, 1)
            pe.wait_ge(s_blk, 1)
            pe.wait_ge(s_edges, 16 * 9)
            for c in range(CHUNKS):
                pe.wait_ge(s_pick, 2 * (c + 1))
                for a in range(3):
                    edges = ends[:, a, c, :] if a < 2 else loaded[:, 2, c, :]
                    for v in range(2):
                        last = nc.tensor.matmul(ps[:, 2 * a + v, 0:HV], edges, pick[:, c % 2, 0, v * HV:(v + 1) * HV],
                                                start=c == 0, stop=c == CHUNKS - 1)
                last.then_inc(s_picked, 1)
            pe.wait_ge(s_visit, 4)

            def pq_step(q, k):
                if live(q, BLOCKS):
                    pe.wait_ge(s_xload[k], (q // XSLOTS + 1) * 32)
                    if later(q, 2):
                        pe.wait_ge(s_xtev, q - 1)
                    for h in range(H):
                        last = nc.tensor.transpose(ps[:, PZ + k % 2, h * P:h * P + NB],
                                                   pxin[:, k, h * P:(h + 1) * P], ident[0:NB, 0:NB])
                    last.then_inc(s_xt, 1)
                if live(q - 1, BLOCKS):
                    o = (k - 1) % 2
                    pe.wait_ge(s_xtev, q)
                    if later(q - 1, 2):
                        pe.wait_ge(s_qr, q - 2)
                    for h in range(H):
                        last = nc.tensor.matmul(ps[0:NB, PM + o, :], pcol[:, o, h, 0:NB], w1[:, h:2 * H:H, :],
                                                start=h == 0, stop=h == H - 1)
                    last.then_inc(s_pqmm, 1)
            steps(pe, BLOCKS, 1, pq_step, by=XSLOTS, slots=XSLOTS)

            s = e[0]

            def hot_columns(q, par):
                pe.wait_ge(s["hot"], q + 1)
                if later(q, 1):
                    pe.wait_ge(s["hev"], q)
                for u in range(QT):
                    last = nc.tensor.transpose(psh[:, u, :], hot[:, par, u, :], identh[:, :])
                last.then_inc(s["hott"], 1)

            def keys(q, par):
                pe.wait_ge(s["keys"], q + 1)
                if later(q, 1):
                    pe.wait_ge(s["same"], q)
                for u in range(QT):
                    for i in range(2):
                        last = nc.tensor.matmul(ps[:, PK, u * P:(u + 1) * P],
                                                keyh[:, par, i, u:u + 1].to_broadcast([P, P]), identh[:, :],
                                                start=i == 0, stop=i == 1)
                last.then_inc(s["keyt"], 1)

            def sum_same(q, par):
                pe.wait_ge(s["same"], q + 1)
                pe.wait_ge(s["msg"], q + 1)
                for u in range(QT):
                    last = nc.tensor.matmul(ps[:, PM + u // 2, u % 2 * D:(u % 2 + 1) * D],
                                            same[:, par, u, :], msg[:, par, u, 0:D], start=True, stop=True)
                last.then_inc(s["ded"], 1)

            def norm_columns(q, par):
                pe.wait_ge(s["norm"], q + 1)
                if later(q, 1):
                    pe.wait_ge(s["zev"], 2 * q)
                for h in range(H):
                    for u in range(QT):
                        last = nc.tensor.transpose(ps[:, PZ + h, u * P:(u + 1) * P],
                                                   act[:, par, u, h * P:(h + 1) * P], ident[:, :])
                    last.then_inc(s["ztr"], 1)

            block_regs = [pe.alloc_register(f"pe_block{u}") for u in range(QT)]

            def expand(q, par, blocks_):
                pe.wait_ge(s["hev"], q + 1)
                if later(q, 1):
                    pe.wait_ge(s["pre"], 2 * q)
                for u in range(QT):
                    for i in range(PARTS):
                        last = nc.tensor.matmul(ps[:, PP + u // 2, u % 2 * D:(u % 2 + 1) * D], hott[:, par, u, :],
                                                big[:, bass.ds(blocks_[u], 1), i, :].rearrange("p a d -> p (a d)"),
                                                start=i == 0, stop=i == PARTS - 1)
                last.then_inc(s["qexp"], 1)

            def main(q, par):
                pe.wait_ge(s["zev"], 2 * (q + 1))
                if later(q, 1):
                    pe.wait_ge(s["tot"], q)
                for u in range(QT):
                    to = ps[:, PM + u // 2, u % 2 * D:(u % 2 + 1) * D]
                    for h in range(H):
                        nc.tensor.matmul(to, zt[:, par, h, u * P:(u + 1) * P], w2[:, h, :], start=h == 0, stop=False)
                    last = nc.tensor.matmul(to, ones[:, :], b2r[:, :], start=False, stop=True)
                last.then_inc(s["mm"], 1)

            def step_0(q, par):
                if live(q + 1, QUADS):
                    of = visit_blocks(pe, q + 1, block_regs)
                if live(q - 1, QUADS):
                    norm_columns(q - 1, 1 - par)
                if live(q - 2, QUADS):
                    sum_same(q - 2, par)
                if live(q + 1, QUADS):
                    expand(q + 1, 1 - par, of)
                if live(q, QUADS):
                    keys(q, par)
                if live(q - 1, QUADS):
                    main(q - 1, 1 - par)
                if live(q + 2, QUADS):
                    hot_columns(q + 2, par)
            pe.wait_ge(s_bias, 6)
            pe.wait_ge(s_wrow, 16)
            pe.wait_ge(s_q3, BLOCKS)
            steps(pe, QUADS, 2, step_0, ahead=2, by=4)

            t = k[0]

            def columns(q, par):
                pe.wait_ge(t["xcopy"], q + 1)
                pe.wait_ge(t["agg"], q + 1)
                if later(q, 2):
                    pe.wait_ge(t["colev"], q - 1)
                for c in range(2 * H):
                    part = (xin[0:NB, par, c * P:(c + 1) * P] if c < H
                            else agg[0:NB, par, (c - H) * P:(c - H + 1) * P])
                    last = nc.tensor.transpose(ps[:, PZ + par, c * P:c * P + NB], part, ident[0:NB, 0:NB])
                last.then_inc(t["cols"], 1)

            def hidden(q, par):
                pe.wait_ge(t["colev"], q + 1)
                if later(q, 2):
                    pe.wait_ge(t["hpre"], q - 1)
                for c in range(2 * H):
                    last = nc.tensor.matmul(ps[0:NB, PM + par, 0:D], col[:, par, c, 0:NB], u1[:, c, :],
                                            start=c == 0, stop=c == 2 * H - 1)
                last.then_inc(t["hmm"], 1)

            def hidden_columns(q, par):
                pe.wait_ge(t["hid"], q + 1)
                if later(q, 2):
                    pe.wait_ge(t["hcolev"], q - 1)
                for h in range(H):
                    last = nc.tensor.transpose(ps[:, PP + par, h * P:h * P + NB],
                                               hid[0:NB, par, h * P:(h + 1) * P], ident[0:NB, 0:NB])
                last.then_inc(t["hcols"], 1)

            def update(q, par):
                pe.wait_ge(t["hcolev"], q + 1)
                if later(q, 1):
                    pe.wait_ge(t["oadd"], q)
                for h in range(H):
                    last = nc.tensor.matmul(ps[0:NB, PK, par * D:(par + 1) * D], hcol[:, par, h, 0:NB], u2[:, h, :],
                                            start=h == 0, stop=h == H - 1)
                last.then_inc(t["omm"], 1)

            def block_0(q, par):
                if live(q, BLOCKS):
                    columns(q, par)
                if live(q - 1, BLOCKS):
                    hidden(q - 1, 1 - par)
                if live(q - 3, BLOCKS):
                    hidden_columns(q - 3, 1 - par)
                if live(q - 4, BLOCKS):
                    update(q - 4, par)
            steps(pe, BLOCKS, 4, block_0, by=4)

            def aggregate(q, par):
                pe.wait_ge(e[1]["hot"], q + 1)
                pe.wait_ge(e[1][f"gat{par}"], half_count(q) * (16 * QT))
                for u in range(QT):
                    if later(q, 1):
                        pe.wait_ge(e[1]["acc"], (q - 1) * QT + u + 1)
                    nc.tensor.matmul(ps[0:NB, u, 0:CW], same[:, par, u, 0:NB], msg[:, par, u, 0:CW],
                                     start=True, stop=True).then_inc(e[1]["agg"], 1)
            pe.wait_ge(s_ones, 1)
            steps(pe, QUADS, 0, aggregate, by=4)

            t = k[1]

            def columns_1(q, par):
                pe.wait_ge(t["agg"], q + 1)
                if later(q, 2):
                    pe.wait_ge(t["colev"], q - 1)
                for c in range(H):
                    last = nc.tensor.transpose(ps[:, PZ + par, c * P:c * P + NB],
                                               agg[0:NB, par, c * P:(c + 1) * P], ident[0:NB, 0:NB])
                last.then_inc(t["cols"], 1)

            def project(q, par):
                pe.wait_ge(t["colev"], q + 1)
                if later(q, 2):
                    pe.wait_ge(t["oadd"], q - 1)
                for c in range(H):
                    last = nc.tensor.matmul(ps[0:NB, PM + par, 0:D], col[:, par, c, 0:NB], wt[:, c, :],
                                            start=c == 0, stop=c == H - 1)
                last.then_inc(t["omm"], 1)

            def block_1(q, par):
                if live(q, BLOCKS):
                    columns_1(q, par)
                if live(q - 1, BLOCKS):
                    project(q - 1, 1 - par)
            steps(pe, BLOCKS, 1, block_1, by=4)

        @block.scalar
        def _(ac):
            ac.wait_ge(s_wtr, 1)
            nc.scalar.activation(flat(wt[:, :, :]), ps[:, PK, :], ACT.Copy).then_inc(s_wt, 1)

            def pq_step(q, par):
                if live(q, BLOCKS):
                    ac.wait_ge(s_xt, q + 1)
                    if later(q, 2):
                        ac.wait_ge(s_pqmm, q - 1)
                    nc.scalar.activation(pcol[:, par, :, 0:NB],
                                         ps[:, PZ + par, 0:H * P].rearrange("p (h n) -> p h n", h=H)[:, :, 0:NB],
                                         ACT.Copy).then_inc(s_xtev, 1)
                if live(q - 1, BLOCKS):
                    ac.wait_ge(s_prow, q)
                    ac.sem_inc(s_turn_act, 1)
                    nc.scalar.activation(big[0:NB, bass.ds(q - 1, 1), 0, :].rearrange("p a d -> p (a d)"),
                                         ps[0:NB, PM + 1 - par, D:2 * D], ACT.Copy).then_inc(s_q1, 1)
                if live(q - 2, BLOCKS):
                    ac.wait_ge(s_qr, q - 1)
                    ac.sem_inc(s_turn_act, 1)
                    nc.scalar.activation(big[0:NB, bass.ds(q - 2, 1), 1, :].rearrange("p a d -> p (a d)"),
                                         qres[:, par, :], ACT.Copy).then_inc(s_q2, 1)
            steps(ac, BLOCKS, 2, pq_step, by=4)

            s = e[0]

            def hot_columns(q, par):
                ac.wait_ge(s["hott"], q + 1)
                if later(q, 2):
                    ac.wait_ge(s["qexp"], q - 1)
                nc.scalar.activation(hott[:, par, :, :], psh[:, :, :], ACT.Copy).then_inc(s["hev"], 1)

            def silu(q, par, v):
                ac.wait_ge(s["pre"], 2 * q + v + 1)
                nc.scalar.activation(act[:, par, 2 * v:2 * v + 2, :], act[:, par, 2 * v:2 * v + 2, :], ACT.Silu)\
                    .then_inc(s["silu"], 1)

            def compare(q, par):
                ac.wait_ge(s["keyt"], q + 1)
                if later(q, 2):
                    ac.wait_ge(s["ded"], q - 1)
                    ac.wait_ge(s["dup"], QT * (q - 1))
                for u in range(QT):
                    nc.scalar.activation(same[:, par, u, :], ps[:, PK, u * P:(u + 1) * P], ACT.Square,
                                         bias=key[:, par, u:u + 1], scale=-1.0).then_inc(s["apart"], 1)
                ac.wait_ge(s["apart"], QT * (q + 1))
                nc.scalar.activation(same[:, par, :, :], same[:, par, :, :], ACT.Relu, bias=onesf[:, 0:1], scale=-1.0)\
                    .then_inc(s["same"], 1)

            def norm_columns(q, par, h):
                ac.wait_ge(s["ztr"], 2 * q + h + 1)
                if h == 0 and later(q, 2):
                    ac.wait_ge(s["mm"], q - 1)
                nc.scalar.activation(zt[:, par, h, :], ps[:, PZ + h, :], ACT.Identity,
                                     bias=gb[:, h, 1:2], scale=gb[:, h, 0:1]).then_inc(s["zev"], 1)

            def message(q, par):
                ac.wait_ge(s["mm"], q + 1)
                if later(q, 2):
                    ac.wait_ge(s["ded"], q - 1)
                nc.scalar.activation(msg[:, par, :, 0:D],
                                     ps[:, PM:PM + 2, :].rearrange("p b (u d) -> p (b u) d", u=2), ACT.Silu)\
                    .then_inc(s["msg"], 1)

            def total(q, par):
                ac.wait_ge(s["ded"], q + 1)
                if later(q, 2):
                    ac.wait_ge(s["added"], (q - 1) * (16 * QT))
                nc.scalar.activation(tot[:, par, :, :],
                                     ps[:, PM:PM + 2, :].rearrange("p b (u d) -> p (b u) d", u=2), ACT.Copy)\
                    .then_inc(s["tot"], 1)

            def step_0(q, par):
                for i in range(2):
                    if live(q, QUADS):
                        silu(q, par, i)
                    if live(q - 1, QUADS):
                        norm_columns(q - 1, 1 - par, i)
                if live(q - 2, QUADS):
                    total(q - 2, par)
                if live(q, QUADS):
                    compare(q, par)
                if live(q - 1, QUADS):
                    message(q - 1, 1 - par)
                if live(q + 2, QUADS):
                    hot_columns(q + 2, par)
            ac.wait_ge(s_weights, 16 * 15)
            steps(ac, QUADS, 2, step_0, ahead=2, by=4)

            t = k[0]

            def block_0(q, par):
                if live(q, BLOCKS):
                    ac.wait_ge(t["cols"], q + 1)
                    if later(q, 2):
                        ac.wait_ge(t["hmm"], q - 1)
                    nc.scalar.activation(col[:, par, :, 0:NB],
                                         ps[:, PZ + par, :].rearrange("p (h n) -> p h n", n=P)[:, :, 0:NB],
                                         ACT.Copy).then_inc(t["colev"], 1)
                if live(q - 2, BLOCKS):
                    ac.wait_ge(t["hpre"], q - 1)
                    if later(q - 2, 2):
                        ac.wait_ge(t["hcols"], q - 3)
                    nc.scalar.activation(hid[0:NB, par, :], hpre[0:NB, par, :], ACT.Silu).then_inc(t["hid"], 1)
                if live(q - 3, BLOCKS):
                    o = 1 - par
                    ac.wait_ge(t["hcols"], q - 2)
                    if later(q - 3, 2):
                        ac.wait_ge(t["omm"], q - 4)
                    nc.scalar.activation(hcol[:, o, :, 0:NB],
                                         ps[:, PP + o, 0:H * P].rearrange("p (h n) -> p h n", n=P)[:, :, 0:NB],
                                         ACT.Copy).then_inc(t["hcolev"], 1)
            steps(ac, BLOCKS, 3, block_0, by=4)

            t = k[1]

            def block_1(q, par):
                ac.wait_ge(t["cols"], q + 1)
                if later(q, 2):
                    ac.wait_ge(t["omm"], q - 1)
                nc.scalar.activation(col[:, par, 0:H, 0:NB],
                                     ps[:, PZ + par, 0:H * P].rearrange("p (h n) -> p h n", n=P)[:, :, 0:NB],
                                     ACT.Copy).then_inc(t["colev"], 1)
            steps(ac, BLOCKS, 0, block_1, by=4)

        @block.vector
        def _(dve):
            def split(first, rest, parts, sem_, at):
                left = [first, *rest]
                nc.vector.tensor_copy(parts[0], first).then_inc(sem_, 1)
                for i in range(PARTS - 1):
                    dve.wait_ge(sem_, at + 2 * i + 1)
                    nc.vector.tensor_tensor(left[i + 1], left[i], parts[i], ALU.subtract).then_inc(sem_, 1)
                    dve.wait_ge(sem_, at + 2 * i + 2)
                    nc.vector.tensor_copy(parts[i + 1], left[i + 1]).then_inc(sem_, 1)

            dve.wait_ge(s_edges, 16 * 9)
            nc.vector.tensor_copy(ends[:, :, :, :], loaded[:, 0:2].bitcast(i32)).then_inc(s_ends, 1)
            dve.wait_ge(s_ends, 1)
            dve.wait_ge(s_const, 10)

            def find_ranges(sems_, at):
                ends_, tile, prev, range_ = sems_
                nc.vector.tensor_reduce(out=thi[:, 0, :], in_=ends[:, 1], axis=AX.X, op=ALU.min).then_inc(tile, 1)
                nc.vector.tensor_reduce(out=thi[:, 1, :], in_=ends[:, 1], axis=AX.X, op=ALU.max).then_inc(tile, 1)
                dve.wait_ge(tile, 2)
                nc.vector.tensor_scalar(thi[:, 0:2, :], thi[:, 0:2, :], 1.0 / NB, (NB - 1) / (2.0 * NB),
                                        ALU.mult, ALU.subtract).then_inc(tile, 1)
                dve.wait_ge(tile, 3)
                nc.vector.tensor_scalar(thi[:, 0:2, :], thi[:, 0:2, :], ROUND, None, ALU.add).then_inc(ends_, 1)
                dve.wait_ge(ends_, at + 1)
                nc.vector.tensor_scalar(thi[:, 2:4, :], thi[:, 0:2, :], ROUND, float(BLOCKS - 1), ALU.subtract, ALU.min)\
                    .then_inc(tile, 1)
                dve.wait_ge(tile, 4)
                nc.vector.scalar_tensor_tensor(out=next_v[:, :], in0=thi[:, 3, :], scalar=1.0, in1=tnum[:, :],
                                               op0=ALU.add, op1=ALU.add).then_inc(range_, 1)
                dve.wait_ge(prev, 1)
                nc.vector.tensor_tensor(first_v[:, :], ps[:, PK, 0:CHUNKS], tnum[:, :], ALU.add).then_inc(range_, 1)
                dve.wait_ge(range_, 2)

            nc.vector.tensor_copy(viota[:, :], viota_i[:, :]).then_inc(s_ends, 1)
            find_ranges((s_ends, s_tile, s_prev, s_range), 2)
            nc.vector.tensor_tensor(down[:, 0:CHUNKS], ps[:, PK, 0:CHUNKS], thi[:, 2, :], ALU.is_gt).then_inc(s_down, 1)
            dve.wait_ge(s_down, 1)
            nc.vector.tensor_reduce(out=down[:, CHUNKS:CHUNKS + 1], in_=down[:, 0:CHUNKS], axis=AX.X, op=ALU.add)\
                .then_inc(s_down, 1)
            dve.wait_ge(s_down, 3)
            nc.vector.tensor_copy(down_i[:, :], ps[:, PP, 0:1]).then_inc(s_flag, 1)
            with dve.If(tiles_down(dve) > 0):
                flat_dst = ends[:, 1].rearrange("p k e -> p (k e)")
                nc.vector.tensor_scalar(f_blk, flat_dst, 1.0 / NB, (NB - 1) / (2.0 * NB), ALU.mult, ALU.subtract)\
                    .then_inc(f_back, 1)
                dve.wait_ge(f_back, 1)
                nc.vector.tensor_scalar(f_blk, f_blk, ROUND, None, ALU.add).then_inc(f_back, 1)
                dve.wait_ge(f_back, 2)
                nc.vector.tensor_scalar(f_blk, f_blk, ROUND, None, ALU.subtract).then_inc(f_back, 1)
                nc.vector.memset(f_run[:, :], 0.0).then_inc(f_back, 1)
                nc.vector.memset(f_pos, 0.0).then_inc(f_back, 1)
                for a, whole in enumerate((ends[:, 0], ends[:, 1], loaded[:, 2])):
                    nc.vector.tensor_copy(f_rec[:, :, a], whole.rearrange("p k e -> p (k e)")).then_inc(f_ready, 1)
                dve.wait_ge(f_back, 5)
                shifts = [1 << i for i in range(W_ALL.bit_length())]
                assert len(shifts) % 2 == 0 and shifts[-1] < W_ALL
                SEQ = 1 + 2 * len(shifts) + 5

                def block_places(q):
                    n = [0]

                    def then(instruction):
                        instruction.then_inc(f_seq, 1)
                        n[0] += 1
                        dve.wait_ge(f_seq, q * SEQ + n[0])
                    then(nc.vector.tensor_scalar(f_mask, f_blk, viota[:, bass.ds(q, 1)], None, ALU.is_equal))
                    for i, d in enumerate(shifts):
                        fr, to = f_mask if i == 0 else f_cum[i % 2], f_cum[(i + 1) % 2]
                        then(nc.vector.tensor_copy(to[:, 0:d], fr[:, 0:d]))
                        then(nc.vector.tensor_tensor(to[:, d:], fr[:, d:], fr[:, 0:W_ALL - d], ALU.add))
                    dve.sem_inc(f_count, 1)
                    dve.wait_ge(f_based, q + 1)
                    then(nc.vector.scalar_tensor_tensor(out=f_run[:, 1:2], in0=ps[:, PZ, 0:1], scalar=-1.0,
                                                        in1=f_run[:, 0:1], op0=ALU.add, op1=ALU.add))
                    then(nc.vector.tensor_tensor(f_run[:, 0:1], ps[:, PZ, 1:2], f_run[:, 0:1], ALU.add))
                    then(nc.vector.tensor_scalar(f_cum[1], f_cum[0], f_run[:, 1:2], None, ALU.add))
                    then(nc.vector.tensor_tensor(f_cum[0], f_cum[1], f_mask, ALU.mult))
                    then(nc.vector.tensor_tensor(f_pos, f_pos, f_cum[0], ALU.add))
                with dve.Fori(0, BLOCKS + 1) as q:
                    block_places(q)
                nc.vector.tensor_copy(f_pos_i, f_pos).then_inc(f_ready, 1)
                dve.wait_ge(f_ready, 4)
                dve.sem_inc(f_ready, 1)
                dve.wait_ge(f_load, 16)
                for a, whole in enumerate((ends[:, 0], ends[:, 1], loaded[:, 2])):
                    nc.vector.tensor_copy(whole.rearrange("p k e -> p (k e)"),
                                          f_sorted.rearrange("p (c a) -> p c a", a=3)[:, :, a]).then_inc(f_ends, 1)
                dve.wait_ge(f_ends, 3)
                find_ranges((f_ends, f_tile, f_prev, f_range), 3)
            HV = VISITS // 2
            for c in range(CHUNKS):
                if c >= 2:
                    dve.wait_ge(s_count, c - 1)
                nc.vector.tensor_scalar(pick[:, c % 2, 0, :], viota[:, :], next_v[:, c:c + 1], None, ALU.is_ge)\
                    .then_inc(s_done_g, 1)
            dve.wait_ge(s_count, CHUNKS)
            nc.vector.tensor_tensor(vdst[:, :].rearrange("p (a v) -> p a v", a=2),
                                    viota[:, :].rearrange("p (a v) -> p a v", a=2), ps[:, 0:2, 0:HV], ALU.subtract)\
                .then_inc(s_blk, 1)
            for c in range(CHUNKS):
                if c >= 2:
                    dve.wait_ge(s_picked, c - 1)
                nc.vector.tensor_scalar(pick[:, c % 2, 1, :], viota[:, :], next_v[:, c:c + 1], None, ALU.is_ge)\
                    .then_inc(s_pick, 1)
                dve.wait_ge(s_pick, 2 * c + 1)
                nc.vector.scalar_tensor_tensor(out=pick[:, c % 2, 0, :], in0=viota[:, :], scalar=first_v[:, c:c + 1],
                                               in1=pick[:, c % 2, 1, :], op0=ALU.is_ge, op1=ALU.subtract)\
                    .then_inc(s_pick, 1)
            dve.wait_ge(s_blk, 1)
            nc.vector.tensor_copy(vblk[:, :], vdst[:, :]).then_inc(s_blk, 1)
            dve.wait_ge(s_picked, CHUNKS)

            def picked(a):
                return ps[:, 2 * a:2 * a + 2, 0:HV]

            def halves(ap):
                return ap.rearrange("p (a v) -> p a v", a=2)
            nc.vector.tensor_copy(halves(vsrc[:, :]), picked(0)).then_inc(s_visit, 1)
            nc.vector.tensor_copy(halves(vkey[:, :]), picked(0)).then_inc(s_visit, 1)
            nc.vector.scalar_tensor_tensor(out=halves(vloc[:, :]), in0=halves(vdst[:, :]), scalar=float(-NB),
                                           in1=picked(1), op0=ALU.mult, op1=ALU.add).then_inc(s_visit, 1)
            nc.vector.tensor_copy(halves(wrest[:, 0, :]), picked(2)).then_inc(s_visit, 1)
            dve.wait_ge(s_visit, 4)
            nc.vector.tensor_scalar(pick[:, 0, 0, :], vloc[:, :], 0.0, None, ALU.is_ge).then_inc(s_visit, 1)
            dve.wait_ge(s_visit, 5)
            nc.vector.scalar_tensor_tensor(out=pick[:, 0, 1, :], in0=vloc[:, :], scalar=float(NB), in1=pick[:, 0, 0, :],
                                           op0=ALU.is_lt, op1=ALU.mult).then_inc(s_visit, 1)
            dve.wait_ge(s_visit, 6)
            nc.vector.scalar_tensor_tensor(out=pick[:, 1, 0, :], in0=vkey[:, :], scalar=float(-PAD),
                                           in1=pick[:, 0, 1, :], op0=ALU.add, op1=ALU.mult).then_inc(s_visit, 1)
            dve.wait_ge(s_visit, 7)
            nc.vector.tensor_scalar(vkey[:, :], pick[:, 1, 0, :], float(PAD), None, ALU.add).then_inc(s_visit, 1)
            dve.wait_ge(s_visit, 8)
            nc.vector.tensor_copy(vkeyh[:, 0, :], vkey[:, :]).then_inc(s_visit, 1)
            dve.wait_ge(s_visit, 9)
            nc.vector.tensor_tensor(vkeyh[:, 1, :], vkey[:, :], vkeyh[:, 0, :], ALU.subtract).then_inc(s_visit, 1)
            split(wrest[:, 0, :], [wrest[:, 1, :], viota[:, :]], [vwgt[:, :, i] for i in range(PARTS)], s_visit, 10)
            dve.wait_ge(s_visit, 10 + 2 * PARTS - 1)
            dve.wait_ge(s_weights, 16 * 15)
            split(w1cf[:, 0, :], [w1cf[:, 1, :], w1cf[:, 0, :]], [w1cp[:, i, :] for i in range(PARTS)], s_wpart, 0)
            split(b2f[:, 0, :], [b2f[:, 1, :], b2f[:, 2, :]], [b2p[:, i, :] for i in range(PARTS)], s_bias, 0)
            dve.wait_ge(s_bias, 5)
            nc.vector.tensor_scalar(b2f[:, 0, :], b2p[:, 0, :], ident[:, 0:1], None, ALU.mult).then_inc(s_range, 1)
            dve.wait_ge(s_range, 3)
            nc.vector.scalar_tensor_tensor(out=b2f[:, 1, :], in0=b2p[:, 1, :], scalar=ident[:, 1:2], in1=b2f[:, 0, :],
                                           op0=ALU.mult, op1=ALU.add).then_inc(s_range, 1)
            dve.wait_ge(s_range, 4)
            nc.vector.scalar_tensor_tensor(out=b2r[:, :], in0=b2p[:, 2, :], scalar=ident[:, 2:3], in1=b2f[:, 1, :],
                                           op0=ALU.mult, op1=ALU.add).then_inc(s_bias, 1)

            def pq_step(q, par):
                if live(q, BLOCKS):
                    dve.wait_ge(s_pqmm, q + 1)
                    if later(q, 2):
                        dve.wait_ge(s_pst[par], half_count(q - 2) * 32)
                        dve.wait_ge(s_q3, q - 1)
                    nc.vector.tensor_tensor(prow[:, par, :], ps[0:NB, PM + par, 0:D], b1b[0:NB, :], ALU.add)\
                        .then_inc(s_prow, 1)
                    dve.wait_ge(s_q1, q + 1)
                    nc.vector.tensor_tensor(qres[:, par, :], ps[0:NB, PM + par, D:2 * D],
                                            big[0:NB, bass.ds(q, 1), 0, :].rearrange("p a d -> p (a d)"),
                                            ALU.subtract).then_inc(s_qr, 1)
                if live(q - 1, BLOCKS):
                    o = 1 - par
                    dve.wait_ge(s_q2, q)
                    nc.vector.tensor_tensor(big[0:NB, bass.ds(q - 1, 1), 2, :].rearrange("p a d -> p (a d)"),
                                            qres[:, o, :], big[0:NB, bass.ds(q - 1, 1), 1, :]
                                            .rearrange("p a d -> p (a d)"), ALU.subtract).then_inc(s_q3, 1)
            steps(dve, BLOCKS, 1, pq_step, by=4)

            s = e[0]

            def stage(q, par, l):
                if later(q, 2):
                    dve.wait_ge(e[l][f"gat{par}"], half_count(q - 2) * (16 * QT))
                    dve.sem_inc(s_turn_dve, 1)
                nc.vector.tensor_copy(idx[:, par, :], vsrc[:, bass.ds(q * QT, QT)]).then_inc(e[l]["staged"], 1)

            def stage_keys(q, par):
                if later(q, 2):
                    dve.wait_ge(s["keyt"], q - 1)
                    dve.wait_ge(s["sidx"], q - 1)
                    dve.sem_inc(s_turn_dve, 1)
                nc.vector.tensor_copy(key[:, par, :], vkey[:, bass.ds(q * QT, QT)])
                nc.vector.tensor_copy(keyh[:, par, :, :], vkeyh[:, :, bass.ds(q * QT, QT)]).then_inc(s["keys"], 1)

            def one_hot(q, par, u):
                if u == 0:
                    if later(q, 2):
                        dve.wait_ge(s["hott"], q - 1)
                    dve.wait_ge(s["placed"], q + 1)
                if u < QT:
                    nc.vector.tensor_scalar(hot[:, par, u, 0:NB], nodes[:, :], loc[:, par, u:u + 1], None,
                                            ALU.is_equal)
                else:
                    nc.vector.tensor_copy(hot[:, par, :, NB:P], vwgt[:, bass.ds(q * QT, QT), :]).then_inc(s["hot"], 1)

            def pre(q, par):
                dve.wait_ge(s[f"gat{par}"], half_count(q) * (16 * QT))
                dve.wait_ge(s["qexp"], q + 1)
                if later(q, 2):
                    dve.wait_ge(s["ztr"], 2 * (q - 1))
                for v in range(2):
                    nc.vector.tensor_tensor(act[:, par, 2 * v:2 * v + 2, :],
                                            ps[:, PP + v, :].rearrange("p (u d) -> p u d", u=2),
                                            gat[:, par, 2 * v:2 * v + 2, :], ALU.add).then_inc(s["pre"], 1)

            def norm(q, par, beside):
                for u in range(QT):
                    if u % 2 == 0:
                        beside(u // 2)
                        dve.wait_ge(s["silu"], 2 * q + u // 2 + 1)
                    nc.vector.bn_stats(bst[:, par, u, :], act[:, par, u, :]).then_inc(s["bst"], 1)
                beside(2)
                dve.wait_ge(s["bst"], QT * (q + 1))
                m = mom[:, par]
                nc.vector.tensor_tensor(m[:, 0], bst[:, par, :, 1], bst[:, par, :, 4], ALU.subtract).then_inc(s["mom"], 1)
                nc.vector.tensor_tensor(m[:, 1], bst[:, par, :, 1], bst[:, par, :, 4], ALU.add).then_inc(s["mom"], 1)
                nc.vector.tensor_tensor(m[:, 2], bst[:, par, :, 2], bst[:, par, :, 5], ALU.add).then_inc(s["mom"], 1)
                dve.wait_ge(s["mom"], 7 * q + 1)
                nc.vector.scalar_tensor_tensor(out=m[:, 0], in0=m[:, 0], scalar=0.25, in1=m[:, 0],
                                               op0=ALU.mult, op1=ALU.mult).then_inc(s["mom"], 1)
                dve.wait_ge(s["mom"], 7 * q + 3)
                nc.vector.tensor_scalar(m[:, 2], m[:, 2], 1.0 / D, LN_EPS, ALU.mult, ALU.add).then_inc(s["mom"], 1)
                nc.vector.tensor_scalar(m[:, 4], m[:, 1], 0.5, None, ALU.mult).then_inc(s["mom"], 1)
                beside(3)
                dve.wait_ge(s["mom"], 7 * q + 6)
                nc.vector.tensor_tensor(m[:, 3], m[:, 2], m[:, 0], ALU.add).then_inc(s["mom"], 1)
                beside(4)
                dve.wait_ge(s["mom"], 7 * q + 7)
                inverse_root(dve, m[:, 3], [nwt[:, par, i] for i in range(4)], s["newt"], q * NEWTON_OPS,
                             lambda i: beside(i + 5))
                dve.wait_ge(s["newt"], (q + 1) * NEWTON_OPS)
                for u in range(QT):
                    last = nc.vector.tensor_scalar(act[:, par, u, :], act[:, par, u, :], m[:, 4, u:u + 1],
                                                   nwt[:, par, 3, u:u + 1], ALU.subtract, ALU.mult)
                last.then_inc(s["norm"], 1)

            def count_before(q, par, u):
                if u == 0:
                    dve.wait_ge(s["same"], q + 1)
                    if later(q, 1):
                        dve.wait_ge(s["dup"], QT * q)
                nc.vector.tensor_tensor_reduce(out=scr[:, u, :], in0=same[:, par, u, :], in1=lower[:, :],
                                               scale=1.0, scalar=0.0, op0=ALU.mult, op1=ALU.add,
                                               accum_out=dup[:, par, u:u + 1]).then_inc(s["dup"], 1)

            def sum_rows(q, par, part):
                if part == 0:
                    nc.vector.tensor_tensor(dif[:, par, :, 0], trash[:, :], key[:, par, :], ALU.subtract)\
                        .then_inc(s["dif"], 1)
                elif part == 1:
                    dve.wait_ge(s["dup"], QT * (q + 1))
                    dve.wait_ge(s["dif"], 2 * q + 1)
                    nc.vector.scalar_tensor_tensor(out=dif[:, par, :, 1], in0=dup[:, par, :], scalar=0.5,
                                                   in1=dif[:, par, :, 0], op0=ALU.is_gt, op1=ALU.mult)\
                        .then_inc(s["dif"], 1)
                else:
                    if later(q, 2):
                        dve.wait_ge(s["added"], (q - 1) * (16 * QT))
                    dve.wait_ge(s["dif"], 2 * q + 2)
                    nc.vector.tensor_tensor(sidx[:, par, :], dif[:, par, :, 1], key[:, par, :], ALU.add)\
                        .then_inc(s["sidx"], 1)

            def step_0(q, par):
                o = 1 - par

                def beside(i):
                    if live(q - 1, QUADS):
                        if i == 0:
                            sum_rows(q - 1, o, 0)
                        elif i == 1:
                            count_before(q - 1, o, 0)
                            count_before(q - 1, o, 1)
                        elif 8 < i <= 10:
                            count_before(q - 1, o, i - 7)
                        elif i == 12:
                            sum_rows(q - 1, o, 1)
                        elif i == 14:
                            sum_rows(q - 1, o, 2)
                    if live(q + 2, QUADS):
                        if i == 2:
                            stage(q + 2, par, 0)
                            nc.vector.tensor_copy(loc[:, par, :], vloc[:, bass.ds((q + 2) * QT, QT)])\
                                .then_inc(s["placed"], 1)
                        elif 3 <= i <= 7:
                            one_hot(q + 2, par, i - 3)
                if live(q, QUADS):
                    pre(q, par)
                if live(q, QUADS):
                    stage_keys(q, par)
                    norm(q, par, beside)
                else:
                    for i in range(5 + 2 + 3 * NEWTON):
                        beside(i)
            dve.wait_ge(s_visit, 10 + 2 * PARTS - 1)
            steps(dve, QUADS, 1, step_0, ahead=2, by=4)

            def hidden(q, par):
                dve.wait_ge(t["hmm"], q + 1)
                if later(q, 2):
                    dve.wait_ge(t["hid"], q - 1)
                nc.vector.tensor_tensor(hpre[0:NB, par, :], ps[0:NB, PM + par, 0:D], ub1b[0:NB, :], ALU.add)\
                    .then_inc(t["hpre"], 1)

            def result(q, par, l):
                row = rows[0:NB, bass.ds(q, 1), 0:D].rearrange("p a d -> p (a d)")
                dve.wait_ge(t["omm"], q + 1)
                of = ps[0:NB, PK, par * D:(par + 1) * D] if l == 0 else ps[0:NB, PM + par, 0:D]
                nc.vector.tensor_tensor(hpre2[0:NB, par, :], of,
                                        (ub2b if l == 0 else blb)[0:NB, :], ALU.add).then_inc(t["oadd"], 1)
                dve.wait_ge(t["oadd"], q + 1)
                if l == 0:
                    dve.wait_ge(t["xcopy"], q + 1)
                    nc.vector.scalar_tensor_tensor(out=row, in0=row, scalar=2.0, in1=hpre2[0:NB, par, :],
                                                   op0=ALU.mult, op1=ALU.add).then_inc(t["res"], 1)
                else:
                    dve.wait_ge(t[f"load{par}"], half_count(q) * 16)
                    nc.vector.scalar_tensor_tensor(out=row, in0=hpre2[0:NB, par, :], scalar=0.0, in1=xin[0:NB, par, :],
                                                   op0=ALU.max, op1=ALU.add).then_inc(t["res"], 1)
                dve.wait_ge(t["res"], q + 1)
                dve.sem_inc(s_turn_dve, 1)
                nc.vector.bn_stats(bstb[:, bass.ds(q, 1), :].rearrange("p a d -> p (a d)"), row).then_inc(t["stat"], 1)

            def normalise_all():
                dve.wait_ge(t["stat"], BLOCKS)
                nc.vector.tensor_tensor(momb[:, 0], bstb[:, :, 1], bstb[:, :, 4], ALU.subtract).then_inc(t["mom"], 1)
                nc.vector.tensor_tensor(momb[:, 1], bstb[:, :, 1], bstb[:, :, 4], ALU.add).then_inc(t["mom"], 1)
                nc.vector.tensor_tensor(momb[:, 2], bstb[:, :, 2], bstb[:, :, 5], ALU.add).then_inc(t["mom"], 1)
                dve.wait_ge(t["mom"], 3)
                nc.vector.scalar_tensor_tensor(out=momb[:, 0], in0=momb[:, 0], scalar=0.25, in1=momb[:, 0],
                                               op0=ALU.mult, op1=ALU.mult).then_inc(t["mom"], 1)
                nc.vector.tensor_scalar(momb[:, 1], momb[:, 1], 0.5, None, ALU.mult).then_inc(t["mom"], 1)
                nc.vector.tensor_scalar(momb[:, 2], momb[:, 2], 1.0 / D, LN_EPS, ALU.mult, ALU.add)\
                    .then_inc(t["mom"], 1)
                dve.wait_ge(t["mom"], 6)
                nc.vector.tensor_tensor(momb[:, 2], momb[:, 2], momb[:, 0], ALU.add).then_inc(t["mom"], 1)
                dve.wait_ge(t["mom"], 7)
                inverse_root(dve, momb[:, 2], [nwb[:, i] for i in range(4)], t["newt"], 0)
                dve.wait_ge(t["newt"], NEWTON_OPS)

                def normalise(q):
                    row = rows[0:NB, bass.ds(q, 1), 0:D].rearrange("p a d -> p (a d)")
                    nc.vector.tensor_scalar(row, row, momb[:, 1, bass.ds(q, 1)], nwb[:, 3, bass.ds(q, 1)],
                                            ALU.subtract, ALU.mult).then_inc(t["norm"], 1)
                with dve.Fori(0, BLOCKS // GROUP) as g:
                    for j in range(GROUP):
                        normalise(g * GROUP + j)

            t = k[0]

            def add_tables(q, par):
                dve.wait_ge(t[f"load{par}"], half_count(q) * (16 * TABLES))
                nc.vector.tensor_tensor(half[0:NB, par, :, :], blk[0:NB, par, 0:2, :], blk[0:NB, par, 2:4, :], ALU.add)\
                    .then_inc(t["half"], 1)
                dve.wait_ge(t["half"], q + 1)
                if later(q, 2):
                    dve.wait_ge(t["cols"], q - 1)
                nc.vector.tensor_tensor(agg[0:NB, par, :], half[0:NB, par, 0, :], half[0:NB, par, 1, :], ALU.add)\
                    .then_inc(t["agg"], 1)

            def block_0(q, par):
                if live(q, BLOCKS):
                    add_tables(q, par)
                if live(q - 2, BLOCKS):
                    hidden(q - 2, par)
                if live(q - 5, BLOCKS):
                    result(q - 5, 1 - par, 0)
            steps(dve, BLOCKS, 5, block_0, by=4)
            normalise_all()

            s = e[1]
            nc.vector.memset(msg[:, :, :, D:CW], 1.0).then_inc(s_ones, 1)

            def clear_rows():
                dve.wait_ge(s_x1st, STORES)
                nc.vector.memset(rows[0:NB, :, 0:CW], 0.0).then_inc(s_ones, 1)
                dve.wait_ge(s_ones, 2)

            def one_hot_1(q, par):
                if later(q, 2):
                    dve.wait_ge(s["agg"], QT * (q - 1))
                    dve.sem_inc(s_turn_dve, 1)
                for u in range(QT):
                    last = nc.vector.tensor_scalar(same[:, par, u, 0:NB], nodes[:, :], vloc[:, bass.ds(q * QT + u, 1)],
                                                   None, ALU.is_equal)
                last.then_inc(s["hot"], 1)

            block_regs = [dve.alloc_register(f"dve_block{u}") for u in range(QT)]

            def accumulate(q, par):
                to = visit_blocks(dve, q, block_regs)
                for u in range(QT):
                    row = rows[0:NB, bass.ds(to[u], 1), 0:CW].rearrange("p a d -> p (a d)")
                    dve.wait_ge(s["agg"], q * QT + u + 1)
                    if u > 0 or later(q, 1):
                        dve.wait_ge(s["acc"], q * QT + u)
                    nc.vector.tensor_tensor(row, ps[0:NB, u, 0:CW], row, ALU.add).then_inc(s["acc"], 1)

            def step_1(q, par):
                if live(q + 1, QUADS):
                    one_hot_1(q + 1, 1 - par)
                if live(q + 2, QUADS):
                    stage(q + 2, par, 1)
                if isinstance(q, int) and q == 0:
                    clear_rows()
                if live(q, QUADS):
                    accumulate(q, par)
            steps(dve, QUADS, 0, step_1, ahead=2, by=4)

            t = k[1]

            def mean(q, par):
                sums_ = rows[0:NB, bass.ds(q, 1), 0:D].rearrange("p a d -> p (a d)")
                if later(q, 2):
                    dve.wait_ge(t["cols"], q - 1)
                nc.vector.tensor_scalar(agg[0:NB, par, :], sums_, cnt[:, 1, bass.ds(q, 1)], None, ALU.mult)\
                    .then_inc(t["agg"], 1)

            def block_1(q, par):
                if live(q, BLOCKS):
                    mean(q, par)
                if live(q - 2, BLOCKS):
                    result(q - 2, par, 1)
            dve.wait_ge(s["acc"], QUADS * QT)
            nc.vector.tensor_scalar(cnt[:, 0, :], rows[0:NB, :, D], 1.0, None, ALU.max).then_inc(t["cnt"], 1)
            dve.wait_ge(t["cnt"], 1)
            nc.vector.reciprocal(cnt[:, 1, :], cnt[:, 0, :]).then_inc(t["cnt"], 1)
            dve.wait_ge(t["cnt"], 2)
            steps(dve, BLOCKS, 2, block_1, by=4)
            normalise_all()


_INS = ["x", "src", "dst", "edge_weight1", "L0_gnn_mW1", "L0_gnn_mb1", "L0_gnn_ln_g", "L0_gnn_ln_b", "L0_gnn_mW2",
        "L0_gnn_mb2", "L0_gnn_uW1", "L0_gnn_ub1", "L0_gnn_uW2", "L0_gnn_ub2", "L1_gnn_W", "L1_gnn_b"]


def kernel(**inputs):
    import numpy as _np
    import concourse.bacc as _bacc
    from concourse import mybir as _mybir
    from concourse.bass_utils import run_bass_kernel_spmd as _run

    nc = _bacc.Bacc("TRN2", target_bir_lowering=False, num_devices=1)
    arrays, args = {}, []
    for name in _INS:
        a = _np.ascontiguousarray(inputs[name])
        arrays[f"in_{name}_dram"] = a
        args.append(nc.dram_tensor(f"in_{name}_dram", a.shape, _mybir.dt.from_np(a.dtype), kind="ExternalInput").ap())
    args.append(nc.dram_tensor("out_0_dram", (N, D), _mybir.dt.float32, kind="ExternalOutput").ap())
    gnn(nc, *args)
    r = _run(nc, [arrays], core_ids=[0])
    return r.results[0]["out_0_dram"]
```
